# Optimizing a Trainium2 kernel written in Bass

```python
import numpy as np
import jax
import jax.numpy as jnp

def _softmax(x, axis=-1):
    return jax.nn.softmax(x, axis=axis)

def _gelu(x):
    return jax.nn.gelu(x, approximate=True)

def _silu(x):
    return jax.nn.silu(x)

def _sigmoid(x):
    return jax.nn.sigmoid(x)

def _layernorm(x, axis=-1, eps=1e-05):
    m = jnp.mean(x, axis=axis, keepdims=True)
    v = jnp.var(x, axis=axis, keepdims=True)
    return (x - m) / jnp.sqrt(v + eps)

def _scatter_add(tgt, idx, src, axis=0):
    return tgt.at[idx].add(src)

def _segment_sum(src, seg, n):
    return jax.ops.segment_sum(src, seg, n)
kernel_name = 'mk_conv_preact_d4_conv_nhwc256_r2_0079f7'

def setup_inputs(seed: int=0):
    np.random.seed(seed)
    _w = jnp.asarray

    def _rec_inputs():
        import jax
        import jax.numpy as jnp
        _gk = jax.random.key(seed)
        x = -9.26e-05 + 0.9999 * jax.random.normal(jax.random.fold_in(_gk, 1), (4, 96, 96, 128), jnp.float32)
        return x
    x = _rec_inputs()

    def _L0_conv_setup():
        import jax, jax.numpy as jnp
        import numpy as np
        DIM = 128
        HEADS = 8
        HD = DIM // HEADS
        WS = (8, 8)
        DS = (2, 2)
        SH = (4, 4)
        TW = (WS[0] * DS[0], WS[1] * DS[1])
        SCALE = HD ** (-0.5)
        N = WS[0] * WS[1]

        def _rope2(t):
            G, wh, ww, hd = t.shape
            da = hd // 2
            half = da // 2
            inv = 1.0 / 10000.0 ** (jnp.arange(half, dtype=jnp.float32) / half)

            def cs(n):
                ang = jnp.arange(n, dtype=jnp.float32)[:, None] * inv
                return (jnp.cos(ang), jnp.sin(ang))
            cH, sH = cs(wh)
            cW, sW = cs(ww)

            def rot(u, c, s):
                u1, u2 = (u[..., :half], u[..., half:])
                return jnp.concatenate([u1 * c - u2 * s, u1 * s + u2 * c], axis=-1)
            th = rot(t[..., :da], cH[None, :, None, :], sH[None, :, None, :])
            tw = rot(t[..., da:], cW[None, None, :, :], sW[None, None, :, :])
            return jnp.concatenate([th, tw], axis=-1)

        def _build_mask(H, W):
            img = np.zeros((H, W), dtype=np.float32)
            h_sl = (slice(0, -WS[0]), slice(-WS[0], -SH[0]), slice(-SH[0], None))
            w_sl = (slice(0, -WS[1]), slice(-WS[1], 0), slice(0, None))
            cnt = 0
            for hs in h_sl:
                for wsl in w_sl:
                    img[hs, wsl] = cnt
                    cnt += 1
            nH, nW = (H // TW[0], W // TW[1])
            mw = img.reshape(nH, TW[0], nW, TW[1]).transpose(0, 2, 1, 3).reshape(-1, TW[0], TW[1])
            Bm = mw.shape[0]
            mw = mw.reshape(Bm, WS[0], DS[0], WS[1], DS[1]).transpose(0, 1, 3, 2, 4).reshape(Bm, N, DS[0] * DS[1]).transpose(0, 2, 1).reshape(Bm * DS[0] * DS[1], N)
            am = np.where(mw[:, None, :] != mw[:, :, None], -np.inf, 0.0).astype(np.float32)
            return jnp.asarray(am)
        key = jax.random.key(seed)
        k1, k2, k3 = jax.random.split(key, 3)
        x = jax.random.normal(k1, (4, 96, 96, DIM), dtype=jnp.float32)
        W_qkv = jax.random.normal(k2, (DIM, 3 * DIM), dtype=jnp.float32) * 0.02
        b_qkv = jnp.zeros((3 * DIM,), dtype=jnp.float32)
        W_proj = jax.random.normal(k3, (DIM, DIM), dtype=jnp.float32) * 0.02
        b_proj = jnp.zeros((DIM,), dtype=jnp.float32)
        return {'x': x, 'W_qkv': W_qkv, 'b_qkv': b_qkv, 'W_proj': W_proj, 'b_proj': b_proj}
    _L0_conv_all = _L0_conv_setup()
    _L0_conv_in = {k: v for k, v in _L0_conv_all.items() if k in ('W_qkv', 'b_qkv', 'W_proj', 'b_proj')}
    del _L0_conv_all

    def _L1_conv_setup():
        import jax, jax.numpy as jnp
        import numpy as np
        B, H, W = (32, 56, 56)
        C_IN, C_OUT, GROUPS, K = (128, 128, 32, 3)
        EPS = 1e-05
        key = jax.random.key(seed)
        k1, k2 = jax.random.split(key, 2)
        x = jax.random.normal(k1, (B, H, W, C_IN), dtype=jnp.float32)
        w = jax.random.normal(k2, (K, K, C_IN // GROUPS, C_OUT), dtype=jnp.float32) * 0.05
        b = jnp.zeros((C_OUT,), dtype=jnp.float32)
        gamma = jnp.ones((C_OUT,), dtype=jnp.float32)
        beta = jnp.zeros((C_OUT,), dtype=jnp.float32)
        return {'x': x, 'w': w, 'b': b, 'gamma': gamma, 'beta': beta}
    _L1_conv_all = _L1_conv_setup()
    _L1_conv_in = {k: v for k, v in _L1_conv_all.items() if k in ('w', 'b', 'gamma', 'beta')}
    del _L1_conv_all

    def _L2_conv_setup():
        import jax, jax.numpy as jnp
        import numpy as np
        from jax import lax
        EXPAND = 32
        CHANNELS = 128

        def _conv(A, W, padding):
            return lax.conv_general_dilated(A, W, (1, 1), padding, dimension_numbers=('NHWC', 'HWIO', 'NHWC'))
        key = jax.random.key(seed)
        ks = jax.random.split(key, 7)
        x = jax.random.normal(ks[0], (16, 32, 32, 128), dtype=jnp.float32)
        s = 0.05
        w1 = jax.random.normal(ks[1], (1, 1, CHANNELS, EXPAND), dtype=jnp.float32) * s
        b1 = jax.random.normal(ks[2], (1, 1, 1, EXPAND), dtype=jnp.float32) * s
        w2 = jax.random.normal(ks[3], (3, 3, CHANNELS, EXPAND), dtype=jnp.float32) * s
        b2 = jax.random.normal(ks[4], (1, 1, 1, EXPAND), dtype=jnp.float32) * s
        w3 = jax.random.normal(ks[5], (1, 1, CHANNELS, 1), dtype=jnp.float32) * s
        b3 = jax.random.normal(ks[6], (1, 1, 1, 1), dtype=jnp.float32) * s
        return {'x': x, 'w1': w1, 'b1': b1, 'w2': w2, 'b2': b2, 'w3': w3, 'b3': b3}
    _L2_conv_all = _L2_conv_setup()
    _L2_conv_in = {k: v for k, v in _L2_conv_all.items() if k in ('w1', 'b1', 'w2', 'b2', 'w3', 'b3')}
    del _L2_conv_all

    def _L3_conv_setup():
        import jax, jax.numpy as jnp
        import numpy as np
        from jax import lax
        EXPAND = 32
        CHANNELS = 128

        def _conv(A, W, padding):
            return lax.conv_general_dilated(A, W, (1, 1), padding, dimension_numbers=('NHWC', 'HWIO', 'NHWC'))
        key = jax.random.key(seed)
        ks = jax.random.split(key, 7)
        x = jax.random.normal(ks[0], (16, 32, 32, 128), dtype=jnp.float32)
        s = 0.05
        w1 = jax.random.normal(ks[1], (1, 1, CHANNELS, EXPAND), dtype=jnp.float32) * s
        b1 = jax.random.normal(ks[2], (1, 1, 1, EXPAND), dtype=jnp.float32) * s
        w2 = jax.random.normal(ks[3], (3, 3, CHANNELS, EXPAND), dtype=jnp.float32) * s
        b2 = jax.random.normal(ks[4], (1, 1, 1, EXPAND), dtype=jnp.float32) * s
        w3 = jax.random.normal(ks[5], (1, 1, CHANNELS, 1), dtype=jnp.float32) * s
        b3 = jax.random.normal(ks[6], (1, 1, 1, 1), dtype=jnp.float32) * s
        return {'x': x, 'w1': w1, 'b1': b1, 'w2': w2, 'b2': b2, 'w3': w3, 'b3': b3}
    _L3_conv_all = _L3_conv_setup()
    _L3_conv_in = {k: v for k, v in _L3_conv_all.items() if k in ('w1', 'b1', 'w2', 'b2', 'w3', 'b3')}
    del _L3_conv_all
    return {'x': x, 'L0_conv_W_qkv': _L0_conv_in['W_qkv'], 'L0_conv_b_qkv': _L0_conv_in['b_qkv'], 'L0_conv_W_proj': _L0_conv_in['W_proj'], 'L0_conv_b_proj': _L0_conv_in['b_proj'], 'L1_conv_w': _L1_conv_in['w'], 'L1_conv_b': _L1_conv_in['b'], 'L1_conv_gamma': _L1_conv_in['gamma'], 'L1_conv_beta': _L1_conv_in['beta'], 'L2_conv_w1': _L2_conv_in['w1'], 'L2_conv_b1': _L2_conv_in['b1'], 'L2_conv_w2': _L2_conv_in['w2'], 'L2_conv_b2': _L2_conv_in['b2'], 'L2_conv_w3': _L2_conv_in['w3'], 'L2_conv_b3': _L2_conv_in['b3'], 'L3_conv_w1': _L3_conv_in['w1'], 'L3_conv_b1': _L3_conv_in['b1'], 'L3_conv_w2': _L3_conv_in['w2'], 'L3_conv_b2': _L3_conv_in['b2'], 'L3_conv_w3': _L3_conv_in['w3'], 'L3_conv_b3': _L3_conv_in['b3']}

def reference(x, L0_conv_W_qkv, L0_conv_b_qkv, L0_conv_W_proj, L0_conv_b_proj, L1_conv_w, L1_conv_b, L1_conv_gamma, L1_conv_beta, L2_conv_w1, L2_conv_b1, L2_conv_w2, L2_conv_b2, L2_conv_w3, L2_conv_b3, L3_conv_w1, L3_conv_b1, L3_conv_w2, L3_conv_b2, L3_conv_w3, L3_conv_b3):
    import jax
    import jax.numpy as jnp

    def _L0_conv_ref(x, W_qkv, b_qkv, W_proj, b_proj):
        import jax, jax.numpy as jnp
        import numpy as np
        DIM = 128
        HEADS = 8
        HD = DIM // HEADS
        WS = (8, 8)
        DS = (2, 2)
        SH = (4, 4)
        TW = (WS[0] * DS[0], WS[1] * DS[1])
        SCALE = HD ** (-0.5)
        N = WS[0] * WS[1]

        def _rope2(t):
            G, wh, ww, hd = t.shape
            da = hd // 2
            half = da // 2
            inv = 1.0 / 10000.0 ** (jnp.arange(half, dtype=jnp.float32) / half)

            def cs(n):
                ang = jnp.arange(n, dtype=jnp.float32)[:, None] * inv
                return (jnp.cos(ang), jnp.sin(ang))
            cH, sH = cs(wh)
            cW, sW = cs(ww)

            def rot(u, c, s):
                u1, u2 = (u[..., :half], u[..., half:])
                return jnp.concatenate([u1 * c - u2 * s, u1 * s + u2 * c], axis=-1)
            th = rot(t[..., :da], cH[None, :, None, :], sH[None, :, None, :])
            tw = rot(t[..., da:], cW[None, None, :, :], sW[None, None, :, :])
            return jnp.concatenate([th, tw], axis=-1)

        def _build_mask(H, W):
            img = np.zeros((H, W), dtype=np.float32)
            h_sl = (slice(0, -WS[0]), slice(-WS[0], -SH[0]), slice(-SH[0], None))
            w_sl = (slice(0, -WS[1]), slice(-WS[1], 0), slice(0, None))
            cnt = 0
            for hs in h_sl:
                for wsl in w_sl:
                    img[hs, wsl] = cnt
                    cnt += 1
            nH, nW = (H // TW[0], W // TW[1])
            mw = img.reshape(nH, TW[0], nW, TW[1]).transpose(0, 2, 1, 3).reshape(-1, TW[0], TW[1])
            Bm = mw.shape[0]
            mw = mw.reshape(Bm, WS[0], DS[0], WS[1], DS[1]).transpose(0, 1, 3, 2, 4).reshape(Bm, N, DS[0] * DS[1]).transpose(0, 2, 1).reshape(Bm * DS[0] * DS[1], N)
            am = np.where(mw[:, None, :] != mw[:, :, None], -np.inf, 0.0).astype(np.float32)
            return jnp.asarray(am)
        Bs, H, W, C = x.shape
        nH, nW = (H // TW[0], W // TW[1])
        nWm = nH * nW * DS[0] * DS[1]
        B_ = Bs * nWm
        Bwin = Bs * nH * nW
        mask = _build_mask(H, W)
        qkv = x.reshape(Bs * H * W, C) @ W_qkv + b_qkv
        qkv = qkv.reshape(B_, N, 3, HEADS, HD).transpose(2, 0, 3, 1, 4)
        q, k, v = (qkv[0], qkv[1], qkv[2])
        q = _rope2(q.reshape(-1, WS[0], WS[1], HD)).reshape(B_, HEADS, N, HD)
        k = _rope2(k.reshape(-1, WS[0], WS[1], HD)).reshape(B_, HEADS, N, HD)
        attn = jnp.einsum('bhnd,bhmd->bhnm', q * SCALE, k)
        attn = attn.reshape(Bs, nWm, HEADS, N, N) + mask[None, :, None, :, :]
        attn = jax.nn.softmax(attn, axis=-1).reshape(B_, HEADS, N, N)
        out = jnp.einsum('bhnm,bhmd->bhnd', attn, v)
        out = out.transpose(0, 2, 1, 3).reshape(B_, N, C)
        out = out.reshape(Bwin, DS[0] * DS[1], N, C).transpose(0, 2, 1, 3)
        out = out.reshape(Bwin, WS[0], WS[1], DS[0], DS[1], C).transpose(0, 1, 3, 2, 4, 5).reshape(Bwin, TW[0], TW[1], C)
        out = out.reshape(Bs, nH, nW, TW[0], TW[1], C).transpose(0, 1, 3, 2, 4, 5).reshape(Bs, H, W, C)
        out = jnp.roll(out, shift=(SH[0], SH[1]), axis=(1, 2))
        out = out.reshape(Bs * H * W, C) @ W_proj + b_proj
        return out.reshape(Bs, H, W, C)

    def _L1_conv_ref(x, w, b, gamma, beta):
        import jax, jax.numpy as jnp
        import numpy as np
        B, H, W = (32, 56, 56)
        C_IN, C_OUT, GROUPS, K = (128, 128, 32, 3)
        EPS = 1e-05
        y = jax.lax.conv_general_dilated(x, w, window_strides=(1, 1), padding='SAME', dimension_numbers=('NHWC', 'HWIO', 'NHWC'), feature_group_count=GROUPS) + b
        mean = jnp.mean(y, axis=(0, 1, 2))
        var = jnp.var(y, axis=(0, 1, 2))
        y = (y - mean) * jax.lax.rsqrt(var + EPS) * gamma + beta
        return jax.nn.relu(y)

    def _L2_conv_ref(x, w1, b1, w2, b2, w3, b3):
        import jax, jax.numpy as jnp
        import numpy as np
        from jax import lax
        EXPAND = 32
        CHANNELS = 128

        def _conv(A, W, padding):
            return lax.conv_general_dilated(A, W, (1, 1), padding, dimension_numbers=('NHWC', 'HWIO', 'NHWC'))
        depth_batch = CHANNELS // EXPAND

        def step1(A, i):
            Z = _conv(A, w1, 'VALID') + b1
            A = lax.dynamic_update_slice(A, Z, (0, 0, 0, i * EXPAND))
            return (A, None)

        def step2(A, i):
            Z = _conv(A, w2, 'SAME') + b2
            A = lax.dynamic_update_slice(A, Z, (0, 0, 0, i * EXPAND))
            return (A, None)

        def step3(A, i):
            Z = _conv(A, w3, 'VALID') + b3
            A = lax.dynamic_update_slice(A, Z, (0, 0, 0, i))
            return (A, None)
        A = x
        A, _ = lax.scan(step1, A, jnp.arange(depth_batch))
        A = jax.nn.relu(A)
        A, _ = lax.scan(step2, A, jnp.arange(depth_batch))
        A = jax.nn.relu(A)
        A, _ = lax.scan(step3, A, jnp.arange(CHANNELS))
        return A + x

    def _L3_conv_ref(x, w1, b1, w2, b2, w3, b3):
        import jax, jax.numpy as jnp
        import numpy as np
        from jax import lax
        EXPAND = 32
        CHANNELS = 128

        def _conv(A, W, padding):
            return lax.conv_general_dilated(A, W, (1, 1), padding, dimension_numbers=('NHWC', 'HWIO', 'NHWC'))
        depth_batch = CHANNELS // EXPAND

        def step1(A, i):
            Z = _conv(A, w1, 'VALID') + b1
            A = lax.dynamic_update_slice(A, Z, (0, 0, 0, i * EXPAND))
            return (A, None)

        def step2(A, i):
            Z = _conv(A, w2, 'SAME') + b2
            A = lax.dynamic_update_slice(A, Z, (0, 0, 0, i * EXPAND))
            return (A, None)

        def step3(A, i):
            Z = _conv(A, w3, 'VALID') + b3
            A = lax.dynamic_update_slice(A, Z, (0, 0, 0, i))
            return (A, None)
        A = x
        A, _ = lax.scan(step1, A, jnp.arange(depth_batch))
        A = jax.nn.relu(A)
        A, _ = lax.scan(step2, A, jnp.arange(depth_batch))
        A = jax.nn.relu(A)
        A, _ = lax.scan(step3, A, jnp.arange(CHANNELS))
        return A + x

    def _gn(v, G=32, eps=1e-05):
        B_, H_, W_, C_ = v.shape
        g = v.reshape(B_, H_, W_, G, C_ // G)
        m = jnp.mean(g, axis=(1, 2, 4), keepdims=True)
        s = jnp.var(g, axis=(1, 2, 4), keepdims=True)
        return ((g - m) / jnp.sqrt(s + eps)).reshape(v.shape)

    def _ln_c(v, eps=1e-06):
        m = jnp.mean(v, axis=-1, keepdims=True)
        s = jnp.var(v, axis=-1, keepdims=True)
        return (v - m) / jnp.sqrt(s + eps)

    def _ln_t(v, eps=1e-05):
        m = jnp.mean(v, axis=-1, keepdims=True)
        s = jnp.var(v, axis=-1, keepdims=True)
        return (v - m) / jnp.sqrt(s + eps)

    def _to_tokens(v):
        B_, H_, W_, C_ = v.shape
        return v.reshape(B_, H_ * W_, C_)

    def _from_tokens(t, like):
        return t.reshape(like.shape)
    x = x + _L0_conv_ref(_gn(x), L0_conv_W_qkv, L0_conv_b_qkv, L0_conv_W_proj, L0_conv_b_proj)
    x = x + _L1_conv_ref(_gn(x), L1_conv_w, L1_conv_b, L1_conv_gamma, L1_conv_beta)
    x = x + _L2_conv_ref(_gn(x), L2_conv_w1, L2_conv_b1, L2_conv_w2, L2_conv_b2, L2_conv_w3, L2_conv_b3)
    x = x + _L3_conv_ref(_gn(x), L3_conv_w1, L3_conv_b1, L3_conv_w2, L3_conv_b2, L3_conv_w3, L3_conv_b3)
    return x

_drawn_inputs = setup_inputs


def setup_inputs(seed=0):
    import zlib

    import numpy as np

    out = dict(_drawn_inputs(seed))
    spreads = {'L0_conv_b_qkv': (0.0, 0.557),
     'L0_conv_b_proj': (0.0, 0.1),
     'L1_conv_b': (0.0, 0.8),
     'L1_conv_gamma': (1.0, 0.2),
     'L1_conv_beta': (0.0, 0.1)}
    factors = {'L0_conv_W_qkv': 7.1,
     'L0_conv_W_proj': 3.19,
     'L2_conv_b1': 2.876,
     'L2_conv_b2': 5.518,
     'L3_conv_b1': 3.706,
     'L3_conv_b2': 7.593}
    for name, (base, spread) in spreads.items():
        noise = np.random.default_rng([zlib.crc32(name.encode()), seed]).standard_normal(out[name].shape)
        drawn = base * np.exp(spread * noise) if base else spread * noise
        out[name] = jnp.asarray(drawn.astype(out[name].dtype))
    for name, factor in factors.items():
        out[name] = (out[name] * factor).astype(out[name].dtype)
    return out
```

```python
from contextlib import ExitStack

import numpy as np

import concourse.bass as bass
from concourse import mybir

F32 = mybir.dt.float32
F32R = mybir.dt.float32r
ALU = mybir.AluOpType
ACT = mybir.ActivationFunctionType
AX = mybir.AxisListType

P = 128
SIDE = 96
IMG = SIDE * SIDE
BANK = 512

HEADS, HD, WIN = 8, 16, 64
QUAD = 4 * WIN
ROW_STEPS = SIDE // 16
STEPS = ROW_STEPS * ROW_STEPS
ROLL = 4
FAR = 3.0e38

TR = 4
TILE = TR * SIDE
TILES = IMG // TILE
PITCH = SIDE + 2
R1 = 4
R2 = 3
BODY = 6

C_ID, C_GAVG = 0, 128
C_ONE, C_F1 = 256, 257
T_CQ, T_SQ, T_CK, T_SK, T_LIM, T_END = 0, 64, 128, 192, 256, 320


def n_flags(images):
    return images * TILES // R1, images * TILES // BODY


def constants(images):
    c = np.arange(P)
    n1, n2 = n_flags(images)
    out = np.zeros((P, C_F1 + 2 * n1 + 2 * n2), np.float32)
    out[:, C_ID:C_ID + P] = np.eye(P)
    out[:, C_GAVG:C_GAVG + P] = (c[:, None] // 4 == c[None] // 4) * 0.25
    out[:, C_ONE] = 1.0
    at = C_F1
    for count, tiles in ((n1, R1), (n2, BODY)):
        g = np.arange(count)
        out[:, at:at + count] = g * tiles % TILES != 0
        out[:, at + count:at + 2 * count] = (g + 1) * tiles % TILES != 0
        at += 2 * count
    return out


def attention_tables():
    out = np.zeros((P, T_END), np.float32)
    inv = (1.0 / 10000.0 ** (np.arange(4, dtype=np.float32) / 4)).astype(np.float32)
    c = np.arange(P)
    d = c % HD
    n = np.arange(WIN)
    pos = np.where((d < 8)[:, None], (n // 8)[None], (n % 8)[None]).astype(np.float32)
    ang = (pos * inv[d % 4][:, None]).astype(np.float32)
    sign = np.where(d % 8 < 4, -1.0, 1.0)[:, None]
    cos, sin = np.cos(ang), np.sin(ang) * sign
    out[:, T_CQ:T_CQ + WIN], out[:, T_SQ:T_SQ + WIN] = cos * HD ** -0.5, sin * HD ** -0.5
    out[:, T_CK:T_CK + WIN], out[:, T_SK:T_SK + WIN] = cos, sin
    region = np.array([0, 0, 0, 0, 1, 1, 2, 2])[n // 8]
    out[:, T_LIM:T_LIM + WIN] = np.where(region[c % WIN][:, None] == region[None], FAR, -FAR)
    return out


def wait(eng, sem, n):
    if not isinstance(n, int) or n > 0:
        eng.wait_ge(sem, n)


class Chain:

    def __init__(self, eng, sem):
        self.eng, self.sem, self.n = eng, sem, 0

    def __call__(self, ins):
        self.n += 1
        ins.then_inc(self.sem, 1)
        self.eng.wait_ge(self.sem, self.n)


class Shared:

    def __init__(self, nc, ctx, images):
        self.nc, self.ctx, self.images = nc, ctx, images
        self.tokens = images * IMG
        self.sems = []
        n1, n2 = n_flags(images)
        self.x = self.sb(ctx, "x_res", [P, self.tokens])
        self.const = self.sb(ctx, "const", [P, C_F1 + 2 * n1 + 2 * n2])
        self.stats = self.sb(ctx, "stats", [P, images * TILES * 6])
        self.gscale = self.sb(ctx, "gscale", [P, images])
        self.gshift = self.sb(ctx, "gshift", [P, images])
        self.bank = [ctx.enter_context(nc.psum_tensor(f"bank{i}", [P, BANK], F32)) for i in range(8)]

    def sb(self, ctx, name, shape, dt=F32):
        return ctx.enter_context(self.nc.sbuf_tensor(name, shape, dt))

    def sem(self, name):
        self.sems.append(self.nc.alloc_semaphore(name=name))
        return self.sems[-1]

    def recycle(self):
        self.nc.clear_and_free_semaphores(self.sems)
        self.nc.all_engine_barrier()
        self.sems = []


def is_prologue(q):
    return isinstance(q, int) and q < 2


def split_product(nc, out, w_hi, w_lo, x_hi, x_lo, start=True, stop=True):
    nc.tensor.matmul(out, w_hi, x_hi, start=start, stop=False)
    nc.tensor.matmul(out, w_hi, x_lo, start=False, stop=False)
    return nc.tensor.matmul(out, w_lo, x_hi, start=False, stop=stop)


def as_f32(ap):
    return ap.bitcast(F32)


LOAD_T = 8
LOAD_RING = 3
CHUNKS = 6


def load_stage(sh, x_dram, const_dram):
    nc = sh.nc
    rounds = sh.tokens // (LOAD_RING * LOAD_T * P)
    with ExitStack() as ctx:
        raw = sh.sb(ctx, "load_raw", [P, LOAD_RING, LOAD_T, P])
        const_in = sh.sem("load_const_in")
        raw_in = [sh.sem(f"load_raw_in{i}") for i in range(LOAD_RING)]
        turned, kept, counted = sh.sem("load_turned"), sh.sem("load_kept"), sh.sem("load_counted")
        x_v = x_dram.rearrange("(g i t p) c -> p i t g c", i=LOAD_RING, t=LOAD_T, p=P)
        block = ctx.enter_context(nc.Block())

        @block.sync
        def _(sp):
            sp.dma_start(sh.const[:, :], const_dram).then_inc(const_in, 16)
            with sp.Fori(0, rounds) as g:
                for i in range(LOAD_RING):
                    sp.wait_ge(turned, g * CHUNKS + 2 * i + 2)
                    sp.dma_start(raw[:, i], x_v[:, i, :, bass.ds(g, 1), :].rearrange("p t g c -> p (t g) c"))\
                        .then_inc(raw_in[i], 16)

        @block.tensor
        def _(pe):
            pe.sem_inc(turned, CHUNKS)
            pe.wait_ge(const_in, 16)
            with pe.Fori(0, rounds) as g:
                for n in range(CHUNKS):
                    i, half = n // 2, n % 2
                    if half == 0:
                        pe.wait_ge(raw_in[i], g * 16 + 16)
                    pe.wait_ge(kept, g * CHUNKS + n + 1)
                    for t in range(4):
                        last = nc.tensor.transpose(
                            sh.bank[n][:, t * P:(t + 1) * P], raw[:, i, 4 * half + t, :],
                            sh.const[:, C_ID:C_ID + P])
                    last.then_inc(turned, 1)

        @block.scalar
        def _(act):
            act.sem_inc(kept, CHUNKS)
            with act.Fori(0, rounds) as g:
                for n in range(CHUNKS):
                    chunk = g * CHUNKS + n
                    act.wait_ge(turned, chunk + 1 + CHUNKS)
                    nc.scalar.activation(sh.x[:, bass.ds(chunk * BANK, BANK)], sh.bank[n][:, :],
                                         ACT.Copy).then_inc(kept, 1)

        @block.vector
        def _(dve):
            with dve.Fori(0, rounds) as g:
                for n in range(CHUNKS):
                    chunk = g * CHUNKS + n
                    dve.wait_ge(kept, chunk + 1 + CHUNKS)
                    nc.vector.bn_stats(sh.stats[:, bass.ds(chunk * 6, 6)],
                                       sh.x[:, bass.ds(chunk * BANK, BANK)]).then_inc(counted, 1)


def rsqrt_steps(nc, link, act_sqrt, out, v, t1, t2, eps):
    link(nc.vector.tensor_scalar(t1, v, eps, None, ALU.add))
    act_sqrt(t2, t1)
    link(nc.vector.reciprocal(out, t2))
    link(nc.vector.tensor_tensor(t2, out, out, ALU.mult))
    link(nc.vector.tensor_tensor(t2, t2, t1, ALU.mult))
    link(nc.vector.tensor_scalar(t2, t2, -0.5, 1.5, ALU.mult, ALU.add))
    link(nc.vector.tensor_tensor(out, out, t2, ALU.mult))


def group_norm_stage(sh, tag, chunks):
    nc, B = sh.nc, sh.images
    with ExitStack() as ctx:
        agg = sh.sb(ctx, f"{tag}_agg", [P, B, 2])
        t1, t2, t3 = (sh.sb(ctx, f"{tag}_t{i}", [P, B]) for i in range(3))
        chain, asked, rooted = sh.sem(f"{tag}_chain"), sh.sem(f"{tag}_asked"), sh.sem(f"{tag}_rooted")
        averaged, to_average = sh.sem(f"{tag}_averaged"), sh.sem(f"{tag}_to_average")
        mean_ps, var_ps = sh.bank[0][:, 0:B], sh.bank[1][:, 0:B]
        gavg = sh.const[:, C_GAVG:C_GAVG + P]
        block = ctx.enter_context(nc.Block())

        @block.tensor
        def _(pe):
            pe.wait_ge(to_average, 1)
            nc.tensor.matmul(mean_ps, gavg, t3[:, :], start=True, stop=True).then_inc(averaged, 1)
            pe.wait_ge(to_average, 2)
            nc.tensor.matmul(var_ps, gavg, t2[:, :], start=True, stop=True).then_inc(averaged, 1)

        @block.scalar
        def _(act):
            act.wait_ge(asked, 1)
            nc.scalar.activation(t2[:, :], t1[:, :], ACT.Sqrt).then_inc(rooted, 1)

        @block.vector
        def _(dve):
            link = Chain(dve, chain)
            for b in range(B):
                link(nc.vector.bn_aggr(agg[:, b, :], sh.stats[:, b * chunks * 6:(b + 1) * chunks * 6]))
            nc.vector.tensor_copy(t3[:, :], agg[:, :, 0]).then_inc(to_average, 1)
            dve.wait_ge(averaged, 1)
            link(nc.vector.tensor_copy(sh.gshift[:, 0:B], mean_ps))
            link(nc.vector.tensor_tensor(t1[:, :], t3[:, :], sh.gshift[:, 0:B], ALU.subtract))
            link(nc.vector.tensor_tensor(t1[:, :], t1[:, :], t1[:, :], ALU.mult))
            nc.vector.tensor_tensor(t2[:, :], t1[:, :], agg[:, :, 1], ALU.add).then_inc(to_average, 1)
            dve.wait_ge(averaged, 2)

            def act_sqrt(out, v):
                dve.sem_inc(asked, 1)
                dve.wait_ge(rooted, 1)

            rsqrt_steps(nc, link, act_sqrt, sh.gscale[:, 0:B], var_ps, t1[:, :], t2[:, :], 1e-5)
            link(nc.vector.scalar_tensor_tensor(sh.gshift[:, 0:B], sh.gshift[:, 0:B], -1.0,
                                                sh.gscale[:, 0:B], ALU.mult, ALU.mult))


class BlockRow:

    def __init__(self, b, r, half):
        self.b, self.r, self.half = b, r, half
        self.number = b * ROW_STEPS + r
        self.masked = isinstance(r, int) and r == ROW_STEPS - 1
        self.first = isinstance(b, int) and isinstance(r, int) and b == r == 0

    def starts(self, j):
        return self.first and j == 0

    def ahead(self, j):
        n = self.number * ROW_STEPS + j
        if not (self.masked and j >= ROW_STEPS - 2):
            return self.b, n * QUAD + 2 * QUAD
        if isinstance(self.b, int):
            return 0, (n + 2) % STEPS * QUAD
        return self.b + 1, n * QUAD + 2 * QUAD

    def tile_before(self, i):
        if isinstance(self.r, int) and self.r == 0:
            return (self.b - 1) * TILES + ((ROW_STEPS - 1) * 4 + 1 + i) % TILES
        return self.b * TILES + (self.r - 1) * 4 + 1 + i


def attention_stage(sh, w_dram, b_dram, tables_dram):
    nc, B = sh.nc, sh.images
    with ExitStack() as ctx:
        w = sh.sb(ctx, "at_w", [P, 6 * P])
        w_hi = sh.sb(ctx, "at_w_hi", [P, 4 * P], F32R)
        w_lo = sh.sb(ctx, "at_w_lo", [P, 4 * P], F32R)
        tables = sh.sb(ctx, "at_tables", [P, T_END])
        bias = sh.sb(ctx, "at_bias", [P, 6])
        b_out = sh.sb(ctx, "at_b_out", [P, 1])
        w_v, w_p = w[:, 4 * P:5 * P], w[:, 5 * P:6 * P]
        xn = [sh.sb(ctx, f"at_xn{i}", [P, QUAD]) for i in range(2)]
        xn_hi = [sh.sb(ctx, f"at_xn_hi{i}", [P, QUAD], F32R) for i in range(2)]
        xn_lo = [sh.sb(ctx, f"at_xn_lo{i}", [P, QUAD], F32R) for i in range(2)]
        turn = [sh.sb(ctx, f"at_turn{i}", [P, QUAD]) for i in range(4)]
        q_r = [sh.sb(ctx, f"at_q{i}", [P, QUAD]) for i in range(2)]
        k_r = [sh.sb(ctx, f"at_k{i}", [P, QUAD]) for i in range(2)]
        k_bd = [sh.sb(ctx, f"at_k_bd{i}", [P, HEADS, QUAD]) for i in range(2)]
        v_bd = [sh.sb(ctx, f"at_v_bd{i}", [P, 4, 4, 2 * HD]) for i in range(3)]
        prob = [[sh.sb(ctx, f"at_prob{i}{p}", [P, HEADS, WIN]) for p in range(2)] for i in range(2)]
        prob_t = [sh.sb(ctx, f"at_prob_t{p}", [P, 4, P]) for p in range(2)]
        top = [sh.sb(ctx, f"at_top{p}", [P, HEADS]) for p in range(2)]
        total = [sh.sb(ctx, f"at_total{p}", [P, HEADS]) for p in range(2)]
        inv = [[sh.sb(ctx, f"at_inv{i}{p}", [P, HEADS]) for p in range(2)] for i in range(2)]
        o_buf = [sh.sb(ctx, f"at_o{i}", [P, 16 * SIDE]) for i in range(2)]
        ps_q, ps_k, ps_s, ps_t, ps_p = sh.bank[0], sh.bank[1], sh.bank[3:5], sh.bank[5:7], sh.bank[7]
        ps_v, ps_o = sh.bank[2][:, 0:QUAD], sh.bank[2][:, QUAD:2 * QUAD]

        s = {n: sh.sem(f"at_{n}") for n in (
            "w_in", "w_hi", "w_lo", "bv_done", "b_out", "zeroed", "xn", "xn_hi", "xn_lo", "v", "qkv", "rope",
            "q_r", "k_r", "v_bd", "scores", "limited", "top", "shifted", "exped", "summed", "inv",
            "normed", "turned", "copied", "pv", "o_buf", "projected", "added",
            "counted")}
        kbd_in = [sh.sem(f"at_kbd_in{i}") for i in range(2)]
        last_step = B * STEPS + 2

        def all_steps(eng, prologue, step, tail):
            def steps(row):
                for j in range(ROW_STEPS):
                    step(row.number * ROW_STEPS + j, j, row)

            def rest_of_image(b):
                with eng.Fori(0, 2) as h:
                    steps(BlockRow(b, h * 2 + 1, 1))
                    steps(BlockRow(b, h * 2 + 2, 0))
                steps(BlockRow(b, ROW_STEPS - 1, 1))

            prologue()
            steps(BlockRow(0, 0, 0))
            if B > 1:
                with eng.Fori(0, B - 1) as b:
                    rest_of_image(b)
                    steps(BlockRow(b + 1, 0, 0))
            rest_of_image(B - 1)
            tail(BlockRow(B, 0, 0))

        block = ctx.enter_context(nc.Block())

        @block.sync
        def _(sp):
            sp.dma_start(w[:, :], w_dram).then_inc(s["w_in"], 16)
            sp.dma_start(bias[:, :], b_dram).then_inc(s["w_in"], 16)
            sp.dma_start(tables[:, :], tables_dram).then_inc(s["w_in"], 16)
            sp.wait_ge(s["zeroed"], 5)

            def spread(q, i):
                sp.wait_ge(s["k_r"], q + 1)
                if not is_prologue(q):
                    sp.wait_ge(s["scores"], 2 * q - 2)
                for h in range(HEADS):
                    sp.dma_start(k_bd[i][HD * h:HD * (h + 1), h, :],
                                 k_r[i][HD * h:HD * (h + 1), :]).then_inc(kbd_in[i], 16)

            def prologue():
                spread(0, 0)
                spread(1, 1)

            all_steps(sp, prologue, lambda n, j, row: spread(n + 2, j % 2), lambda row: None)
            sp.wait_ge(kbd_in[0], 128 * (last_step // 2))
            sp.wait_ge(kbd_in[1], 128 * (last_step // 2))

        @block.gpsimd
        def _(pool):
            for i in range(3):
                pool.memset(v_bd[i][:, :, :, :], 0.0).then_inc(s["zeroed"], 1)
            for i in range(2):
                pool.memset(k_bd[i][:, :, :], 0.0).then_inc(s["zeroed"], 1)

            def split_x(q, i):
                pool.wait_ge(s["xn"], q + 1)
                pool.wait_ge(s["xn_hi"], q + 1)
                nc.gpsimd.tensor_tensor(xn_lo[i][:, :], xn[i][:, :], as_f32(xn_hi[i][:, :]),
                                        ALU.subtract).then_inc(s["xn_lo"], 1)

            def add_rope(q, i):
                pool.wait_ge(s["rope"], q + 1)
                if not is_prologue(q):
                    pool.wait_ge(s["scores"], 2 * q - 2)
                nc.gpsimd.tensor_tensor(q_r[i][:, :], turn[0][:, :], turn[1][:, :],
                                        ALU.add).then_inc(s["q_r"], 1)
                if not is_prologue(q):
                    pool.wait_ge(kbd_in[i], (q - i) * 64)
                nc.gpsimd.tensor_tensor(k_r[i][:, :], turn[2][:, :], turn[3][:, :],
                                        ALU.add).then_inc(s["k_r"], 1)

            def prologue():
                for q in range(2):
                    split_x(q, q)
                    add_rope(q, q)

            def step(n, j, row):
                i = j % 2
                split_x(n + 2, i)
                for p in range(2):
                    pool.wait_ge(s["inv"], 2 * n + p + 1)
                    nc.gpsimd.tensor_tensor(
                        prob[i][p][:, :, :], prob[i][p][:, :, :],
                        inv[i][p][:, :].unsqueeze(2).broadcast_to([P, HEADS, WIN]),
                        ALU.mult).then_inc(s["normed"], 1)
                add_rope(n + 2, i)

            all_steps(pool, prologue, step, lambda row: None)

        @block.scalar
        def _(act):
            act.wait_ge(s["w_in"], 48)
            nc.scalar.activation(w_hi[:, :], w[:, 0:4 * P], ACT.Copy).then_inc(s["w_hi"], 1)
            act.wait_ge(s["zeroed"], 3)
            act.sem_inc(s["copied"], 2)
            act.sem_inc(s["o_buf"], 1)

            def normalise_x(q, i, image, col):
                wait(act, s["qkv"], q - 1)
                wait(act, s["v"], q - 1)
                for out, signal in ((xn_hi, "xn_hi"), (xn, "xn")):
                    nc.scalar.activation(out[i][:, :], sh.x[:, bass.ds(col, QUAD)], ACT.Identity,
                                         scale=sh.gscale[:, bass.ds(image, 1)],
                                         bias=sh.gshift[:, bass.ds(image, 1)]).then_inc(s[signal], 1)

            def keep_v(q, k):
                act.wait_ge(s["v"], q + 1)
                if not is_prologue(q):
                    act.wait_ge(s["pv"], q - 1)
                for half in range(2):
                    rows = slice(WIN * half, WIN * (half + 1))
                    out = v_bd[k][rows, :, :, HD * half:HD * (half + 1)]
                    last = nc.scalar.activation(
                        out, ps_v[rows, :].rearrange("p (w h d) -> p w h d", w=4, d=HD), ACT.Copy)
                last.then_inc(s["v_bd"], 1)

            def keep_o(n, half, j):
                act.wait_ge(s["pv"], n + 2)
                o = o_buf[half][:, :].rearrange("p (r e c f) -> p r e c f", e=2, c=SIDE // 2, f=2)
                col = (16 * j + ROLL) // 2
                inside = min(8, SIDE // 2 - col)
                for e in range(2):
                    src = ps_o[:, 2 * WIN * e:2 * WIN * (e + 1)].rearrange("p (f i j) -> p i j f", f=2, j=8)
                    last = nc.scalar.activation(o[:, :, e, col:col + inside, :], src[:, :, 0:inside, :],
                                                ACT.Copy)
                    if inside < 8:
                        last = nc.scalar.activation(o[:, :, e, 0:8 - inside, :], src[:, :, inside:8, :],
                                                    ACT.Copy)
                last.then_inc(s["o_buf"], 1)

            def prologue():
                for q in range(2):
                    normalise_x(q, q, 0, q * QUAD)
                keep_v(0, 0)

            def step(n, j, row):
                normalise_x(n + 2, j % 2, *row.ahead(j))
                for p in range(2):
                    act.wait_ge(s["shifted"], n * 2 + p + 3)
                    nc.scalar.activation(prob[j % 2][p][:, :, :], prob[j % 2][p][:, :, :],
                                         ACT.Exp).then_inc(s["exped"], 1)
                    if p == 0:
                        keep_v(n + 1, (j + 1) % 3)
                    if not row.starts(j):
                        turn_back(n - 1, p)
                if j == 1 and not row.first:
                    act.wait_ge(s["projected"], row.number * 4 - 3)
                if not row.starts(j):
                    keep_o(n - 1, row.half if j else 1 - row.half, (j - 1) % ROW_STEPS)

            def turn_back(n, p):
                act.wait_ge(s["turned"], n * 2 + p + 5)
                act.wait_ge(s["pv"], n + 1)
                nc.scalar.activation(prob_t[p][:, :, :], ps_t[p][:, :].rearrange("p (h n) -> p h n", h=4),
                                     ACT.Copy).then_inc(s["copied"], 1)

            def tail(row):
                n = B * STEPS - 1
                for p in range(2):
                    turn_back(n, p)
                keep_o(n, 1, ROW_STEPS - 1)

            all_steps(act, prologue, step, tail)

        @block.vector
        def _(dve):
            dve.wait_ge(s["w_hi"], 1)
            nc.vector.tensor_tensor(w_lo[:, :], w[:, 0:4 * P], as_f32(w_hi[:, :]),
                                    ALU.subtract).then_inc(s["w_lo"], 1)
            dve.wait_ge(s["bv_done"], 1)
            nc.vector.tensor_tensor(b_out[:, :], ps_p[:, 0:1], bias[:, 5:6], ALU.add).then_inc(s["b_out"], 1)
            dve.sem_inc(s["added"], 1)
            dve.sem_inc(s["shifted"], 2)

            def rope(q):
                dve.wait_ge(s["qkv"], q + 1)
                wait(dve, s["k_r"], q)
                for m in range(4):
                    ps = (ps_q, ps_k)[m // 2][:, m % 2 * QUAD:(m % 2 + 1) * QUAD]
                    at = (T_CQ, T_SQ, T_CK, T_SK)[m]
                    table = tables[:, at:at + WIN].unsqueeze(1).broadcast_to([P, 4, WIN])
                    last = nc.vector.scalar_tensor_tensor(
                        turn[m][:, :].rearrange("p (w n) -> p w n", w=4),
                        ps.rearrange("p (w n) -> p w n", w=4), bias[:, m:m + 1], table, ALU.add, ALU.mult)
                last.then_inc(s["rope"], 1)

            def step(n, j, row):
                i = j % 2
                for p in range(2):
                    dve.wait_ge(s["scores"], 2 * n + p + 1)
                    src = ps_s[p][:, :].rearrange("p (h m) -> p h m", h=HEADS)
                    dve.wait_ge(s["turned"], n * 2 + p + 1)
                    if row.masked:
                        table = tables[:, T_LIM:T_LIM + WIN].unsqueeze(1).broadcast_to([P, HEADS, WIN])
                        nc.vector.tensor_tensor(prob[i][p][:, :, :], src, table, ALU.min).then_inc(s["limited"], 1)
                        src = prob[i][p][:, :, :]
                        dve.wait_ge(s["limited"], row.b * (2 * ROW_STEPS) + 2 * j + p + 1)
                    nc.vector.reduce_max(top[p][:, :], src, AX.X).then_inc(s["top"], 1)
                    dve.wait_ge(s["top"], 2 * n + p + 1)
                    nc.vector.tensor_tensor(
                        prob[i][p][:, :, :], src,
                        top[p][:, :].unsqueeze(2).broadcast_to([P, HEADS, WIN]),
                        ALU.subtract).then_inc(s["shifted"], 1)
                if j >= 2 and not row.first:
                    add_projection(row, j - 2)
                for p in range(2):
                    dve.wait_ge(s["exped"], 2 * n + p + 1)
                    nc.vector.reduce_sum(total[p][:, :], prob[i][p][:, :, :], AX.X).then_inc(s["summed"], 1)
                    dve.wait_ge(s["summed"], 2 * n + p + 1)
                    nc.vector.reciprocal(inv[i][p][:, :], total[p][:, :]).then_inc(s["inv"], 1)
                rope(n + 2)

            def add_projection(row, i):
                t = row.tile_before(i)
                p = row.number * 4 - 4 + i
                dve.wait_ge(s["projected"], p + 2)
                xt = sh.x[:, bass.ds(t * TILE, TILE)]
                nc.vector.scalar_tensor_tensor(xt, ps_p[:, 0:TILE], b_out[:, 0:1], xt,
                                               ALU.add, ALU.add).then_inc(s["added"], 1)
                dve.wait_ge(s["added"], p + 2)
                nc.vector.bn_stats(sh.stats[:, bass.ds(t * 6, 6)], xt).then_inc(s["counted"], 1)

            def tail(row):
                for i in range(4):
                    add_projection(row, i)

            def prologue():
                rope(0)
                rope(1)

            all_steps(dve, prologue, step, tail)

        @block.tensor
        def _(pe):
            pe.wait_ge(s["w_in"], 48)
            nc.tensor.matmul(ps_p[:, 0:1], w_p, bias[:, 4:5], start=True, stop=True).then_inc(s["bv_done"], 1)
            pe.sem_inc(s["turned"], 4)
            pe.sem_inc(s["pv"], 1)
            pe.sem_inc(s["projected"], 1)
            pe.wait_ge(s["w_lo"], 1)
            pe.wait_ge(s["b_out"], 1)

            def project_in(q, i):
                pe.wait_ge(s["xn_hi"], q + 1)
                pe.wait_ge(s["xn_lo"], q + 1)
                wait(pe, s["rope"], q)
                for m in range(4):
                    out = (ps_q, ps_k)[m // 2][:, m % 2 * QUAD:(m % 2 + 1) * QUAD]
                    cols = slice(m * P, (m + 1) * P)
                    last = split_product(nc, out, w_hi[:, cols], w_lo[:, cols], xn_hi[i][:, :],
                                         xn_lo[i][:, :])
                last.then_inc(s["qkv"], 1)

            def project_v(q, i):
                pe.wait_ge(s["xn"], q + 1)
                wait(pe, s["v_bd"], q)
                if not is_prologue(q):
                    pe.wait_ge(s["o_buf"], q - 1)
                for wdw in range(4):
                    for half in range(2):
                        last = nc.tensor.matmul(
                            ps_v[WIN * half:WIN * (half + 1), WIN * wdw:WIN * (wdw + 1)],
                            xn[i][:, WIN * wdw:WIN * (wdw + 1)], w_v[:, WIN * half:WIN * (half + 1)],
                            start=True, stop=True)
                last.then_inc(s["v"], 1)

            def score(n, i):
                pe.wait_ge(s["q_r"], n + 1)
                pe.wait_ge(kbd_in[i], (n - i) * 64 + 128)
                for wdw in range(4):
                    p = wdw // 2
                    if wdw % 2 == 0:
                        pe.wait_ge(s["shifted"], n * 2 + p + 1)
                    rows = slice(WIN * (wdw % 2), WIN * (wdw % 2 + 1))
                    last = nc.tensor.matmul(
                        ps_s[p][rows, :].rearrange("p (h m) -> p h m", h=HEADS),
                        q_r[i][:, WIN * wdw:WIN * (wdw + 1)],
                        k_bd[i][:, :, WIN * wdw:WIN * (wdw + 1)], start=True, stop=True)
                    if wdw % 2:
                        last.then_inc(s["scores"], 1)

            def turn_probs(n, i):
                for p in range(2):
                    pe.wait_ge(s["normed"], n * 2 + p + 1)
                    pe.wait_ge(s["copied"], n * 2 + p + 1)
                    for hp in range(4):
                        last = nc.tensor.transpose(
                            ps_t[p][:, hp * P:(hp + 1) * P],
                            prob[i][p][:, 2 * hp:2 * hp + 2, :].rearrange("p h m -> p (h m)"),
                            sh.const[:, C_ID:C_ID + P])
                    last.then_inc(s["turned"], 1)

            def weigh(n, k):
                pe.wait_ge(s["copied"], n * 2 + 4)
                ahead = min(n + 3, B * STEPS + 1) if isinstance(n, int) else n + 3
                pe.wait_ge(s["v_bd"], ahead)
                pe.wait_ge(s["o_buf"], n + 1)
                for wdw in range(4):
                    for hp in range(4):
                        last = nc.tensor.matmul(
                            ps_o[32 * hp:32 * (hp + 1), WIN * wdw:WIN * (wdw + 1)], v_bd[k][:, wdw, hp, :],
                            prob_t[wdw // 2][:, hp, WIN * (wdw % 2):WIN * (wdw % 2 + 1)],
                            start=True, stop=True)
                last.then_inc(s["pv"], 1)

            def prologue():
                project_in(0, 0)
                project_in(1, 1)
                project_v(0, 0)

            def project(row, i):
                pe.wait_ge(s["o_buf"], row.number * ROW_STEPS + 1)
                pe.wait_ge(s["added"], row.number * 4 - 3 + i)
                nc.tensor.matmul(ps_p[:, 0:TILE], w_p, o_buf[1 - row.half][:, i * TILE:(i + 1) * TILE],
                                 start=True, stop=True).then_inc(s["projected"], 1)

            def step(n, j, row):
                score(n, j % 2)
                project_v(n + 1, (j + 1) % 2)
                if not row.starts(j):
                    turn_probs(n - 1, (j + 1) % 2)
                project_in(n + 2, j % 2)
                if not row.starts(j):
                    weigh(n - 1, (j + 2) % 3)
                if 1 <= j <= 4 and not row.first:
                    project(row, j - 1)

            def tail(row):
                n = B * STEPS - 1
                turn_probs(n, 1)
                weigh(n, 2)
                for i in range(4):
                    project(row, i)

            all_steps(pe, prologue, step, tail)


TAPS = [(dy, dx) for dy in (-1, 0, 1) for dx in (-1, 0, 1)]


def walk_groups(eng, groups, body):
    with eng.Fori(0, groups - 1) as g:
        body(g)
    body(groups - 1)


def group_tables(nc, sh, link, per_image, scale, shift):
    for out, src in ((scale, sh.gscale), (shift, sh.gshift)):
        link(nc.vector.tensor_copy(
            out[:, :].rearrange("p (b g) -> p b g", g=per_image),
            src[:, 0:sh.images].unsqueeze(2).broadcast_to([P, sh.images, per_image])))


def conv1_stage(sh, w_dram, b_dram, y_dram):
    nc = sh.nc
    groups = sh.images * TILES // R1
    tiles = groups * R1
    first_flag, last_flag = (sh.const[:, C_F1 + i * groups:C_F1 + (i + 1) * groups] for i in range(2))
    rows = R1 * TR + 2
    with ExitStack() as ctx:
        w = sh.sb(ctx, "c1_w", [P, 9, P])
        w_hi = sh.sb(ctx, "c1_w_hi", [P, 9, P], F32R)
        w_lo = sh.sb(ctx, "c1_w_lo", [P, 9, P], F32R)
        bias = sh.sb(ctx, "c1_bias", [P, 1])
        scale, shift = (sh.sb(ctx, f"c1_{n}", [P, groups]) for n in ("scale", "shift"))
        xn = [sh.sb(ctx, f"c1_xn{i}", [P, TILE]) for i in range(2)]
        ring_hi = sh.sb(ctx, "c1_ring_hi", [P, rows, PITCH], F32R)
        ring_lo = sh.sb(ctx, "c1_ring_lo", [P, rows, PITCH], F32R)
        y = sh.sb(ctx, "c1_y", [P, R1, TILE])
        s = {n: sh.sem(f"c1_{n}") for n in (
            "w_in", "w_masked", "w_hi", "w_lo", "chain", "xn", "hi", "lo", "mirrored", "conv",
            "y_kept", "counted")}
        y_out = [sh.sem(f"c1_y_out{i}") for i in range(R1)]

        def rows_of(t, j):
            return slice(1 + TR * j, 1 + TR * (j + 1))

        block = ctx.enter_context(nc.Block())

        @block.sync
        def _(sp):
            sp.dma_start(w[:, :, :], w_dram).then_inc(s["w_in"], 16)
            sp.dma_start(bias[:, :], b_dram).then_inc(s["w_in"], 16)
            for i in range(R1):
                sp.sem_inc(y_out[i], 16)
            with sp.Fori(0, groups) as g:
                for j in range(R1):
                    t = g * R1 + j
                    sp.wait_ge(s["y_kept"], t + 1 + R1)
                    sp.dma_start(y_dram[:, bass.ds(t * TILE, TILE)], y[:, j, :]).then_inc(y_out[j], 16)
            for i in range(R1):
                sp.wait_ge(y_out[i], 16 * (groups + 1))

        @block.gpsimd
        def _(pool):
            nc.gpsimd.memset(as_f32(ring_hi[:, :, :]), 0.0)
            nc.gpsimd.memset(as_f32(ring_lo[:, :, :]), 0.0).then_inc(s["mirrored"], 1)

            def mirror(t, g, j):
                if j not in (0, R1 - 1):
                    return
                src, dst, flag = (1, rows - 1, first_flag) if j == 0 else (R1 * TR, 0, last_flag)
                pool.wait_ge(s["hi"], t + 1)
                pool.wait_ge(s["lo"], t + 1)
                for ring in (ring_hi, ring_lo):
                    last = nc.gpsimd.tensor_tensor(ring[:, dst, :], as_f32(ring[:, src, :]),
                                                   flag[:, bass.ds(g, 1)].broadcast_to([P, PITCH]), ALU.mult)
                last.then_inc(s["mirrored"], 1)

            for t in range(2):
                mirror(t, 0, t)

            def body(g):
                for j in range(R1):
                    t = g * R1 + j + 2
                    if not (isinstance(t, int) and t >= tiles):
                        mirror(t, g + (j + 2) // R1, (j + 2) % R1)

            walk_groups(pool, groups, body)
            pool.wait_ge(s["conv"], tiles - 4 + 3)
            nc.gpsimd.memset(as_f32(ring_hi[:, rows - 1, :]), 0.0)
            nc.gpsimd.memset(as_f32(ring_lo[:, rows - 1, :]), 0.0).then_inc(s["mirrored"], 1)

        @block.scalar
        def _(act):
            act.wait_ge(s["w_masked"], 1)
            nc.scalar.activation(w_hi[:, :, :], w[:, :, :], ACT.Copy).then_inc(s["w_hi"], 1)
            act.sem_inc(s["y_kept"], R1)
            act.wait_ge(s["mirrored"], 1)
            act.wait_ge(s["chain"], 2)

            def hi(t, g, j):
                wait(act, s["conv"], t + 1)
                wait(act, s["lo"], t - 1)
                if j == 0:
                    wait(act, s["mirrored"], g * 2)
                nc.scalar.activation(
                    ring_hi[:, rows_of(t, j), 1:1 + SIDE],
                    sh.x[:, bass.ds(t * TILE, TILE)].rearrange("p (r c) -> p r c", c=SIDE),
                    ACT.Identity, scale=scale[:, bass.ds(g, 1)],
                    bias=shift[:, bass.ds(g, 1)]).then_inc(s["hi"], 1)
                nc.scalar.activation(xn[j % 2][:, :], sh.x[:, bass.ds(t * TILE, TILE)], ACT.Identity,
                                     scale=scale[:, bass.ds(g, 1)],
                                     bias=shift[:, bass.ds(g, 1)]).then_inc(s["xn"], 1)

            for t in range(2):
                hi(t, 0, t)

            def body(g):
                for j in range(R1):
                    t = g * R1 + j
                    if not (isinstance(t, int) and t + 2 >= tiles):
                        hi(t + 2, g + (j + 2) // R1, (j + 2) % R1)
                    act.wait_ge(s["conv"], t + 1 + 3)
                    act.wait_ge(y_out[j], g * 16 + 16)
                    act.wait_ge(s["counted"], t + 1)
                    nc.scalar.activation(y[:, j, :], sh.bank[j][:, 0:TILE], ACT.Identity,
                                         bias=bias[:, 0:1]).then_inc(s["y_kept"], 1)

            walk_groups(act, groups, body)

        @block.vector
        def _(dve):
            link = Chain(dve, s["chain"])
            group_tables(nc, sh, link, TILES // R1, scale, shift)
            dve.wait_ge(s["w_in"], 32)
            nc.vector.scalar_tensor_tensor(
                w[:, :, :], w[:, :, :], 4.0,
                sh.const[:, C_GAVG:C_GAVG + P].unsqueeze(1).broadcast_to([P, 9, P]),
                ALU.mult, ALU.mult).then_inc(s["w_masked"], 1)
            dve.wait_ge(s["w_hi"], 1)
            nc.vector.tensor_tensor(w_lo[:, :, :], w[:, :, :], as_f32(w_hi[:, :, :]),
                                    ALU.subtract).then_inc(s["w_lo"], 1)
            dve.sem_inc(s["counted"], R1)

            def lo(t, i, j):
                dve.wait_ge(s["xn"], t + 1)
                dve.wait_ge(s["hi"], t + 1)
                at = (slice(None), rows_of(t, j), slice(1, 1 + SIDE))
                nc.vector.tensor_tensor(
                    ring_lo[at], xn[i][:, :].rearrange("p (r c) -> p r c", c=SIDE),
                    as_f32(ring_hi[:, :, :])[at], ALU.subtract).then_inc(s["lo"], 1)

            for t in range(2):
                lo(t, t, t)

            def body(g):
                for j in range(R1):
                    t = g * R1 + j
                    if not (isinstance(t, int) and t + 2 >= tiles):
                        lo(t + 2, j % 2, (j + 2) % R1)
                    dve.wait_ge(s["y_kept"], t + 1 + R1)
                    nc.vector.bn_stats(sh.stats[:, bass.ds(t * 6, 6)], y[:, j, :]).then_inc(s["counted"], 1)

            walk_groups(dve, groups, body)

        @block.tensor
        def _(pe):
            pe.sem_inc(s["conv"], 3)
            pe.wait_ge(s["w_lo"], 1)

            def body(g):
                for j in range(R1):
                    t = g * R1 + j
                    ready = min(t + 2, tiles) if isinstance(t, int) else t + 2
                    pe.wait_ge(s["hi"], ready)
                    pe.wait_ge(s["lo"], ready)
                    if j == 0:
                        pe.wait_ge(s["mirrored"], g * 2 + 1)
                    if j == R1 - 1:
                        pe.wait_ge(s["mirrored"], g * 2 + 4)
                    pe.wait_ge(s["y_kept"], t + 1)
                    out = sh.bank[j][:, 0:TILE].rearrange("p (r c) -> p r c", c=SIDE)
                    for n, (dy, dx) in enumerate(TAPS):
                        at = (slice(None), slice(1 + TR * j + dy, 1 + TR * (j + 1) + dy),
                              slice(1 + dx, 1 + dx + SIDE))
                        last = split_product(nc, out, w_hi[:, n, :], w_lo[:, n, :], ring_hi[at],
                                             ring_lo[at], start=n == 0, stop=n == 8)
                    last.then_inc(s["conv"], 1)

            walk_groups(pe, groups, body)


APPLY_T = 3
APPLY_RING = 4


def batch_norm_stage(sh, gb_dram, y_dram):
    nc = sh.nc
    tiles = sh.images * TILES
    width = APPLY_T * TILE
    rounds = tiles // (APPLY_T * APPLY_RING)
    with ExitStack() as ctx:
        gb = sh.sb(ctx, "bn_gb", [P, 2])
        agg = sh.sb(ctx, "bn_agg", [P, 2])
        t1, t2, scale, shift = (sh.sb(ctx, f"bn_{n}", [P, 1]) for n in ("t1", "t2", "scale", "shift"))
        y = sh.sb(ctx, "bn_y", [P, APPLY_RING, width])
        s = {n: sh.sem(f"bn_{n}") for n in (
            "gb_in", "chain", "asked", "rooted", "ready", "relu", "added", "counted")}
        y_in = [sh.sem(f"bn_y_in{i}") for i in range(APPLY_RING)]
        block = ctx.enter_context(nc.Block())

        @block.sync
        def _(sp):
            sp.dma_start(gb[:, :], gb_dram).then_inc(s["gb_in"], 16)
            with sp.Fori(0, rounds) as g:
                for j in range(APPLY_RING):
                    n = g * APPLY_RING + j
                    sp.wait_ge(s["added"], n + 1)
                    sp.dma_start(y[:, j, :], y_dram[:, bass.ds(n * width, width)]).then_inc(y_in[j], 16)

        @block.scalar
        def _(act):
            act.wait_ge(s["asked"], 1)
            nc.scalar.activation(t2[:, :], t1[:, :], ACT.Sqrt).then_inc(s["rooted"], 1)
            act.wait_ge(s["ready"], 1)
            with act.Fori(0, rounds) as g:
                for j in range(APPLY_RING):
                    act.wait_ge(y_in[j], g * 16 + 16)
                    nc.scalar.activation(y[:, j, :], y[:, j, :], ACT.Relu, scale=scale[:, 0:1],
                                         bias=shift[:, 0:1]).then_inc(s["relu"], 1)

        @block.vector
        def _(dve):
            link = Chain(dve, s["chain"])
            dve.sem_inc(s["added"], APPLY_RING)
            link(nc.vector.bn_aggr(agg[:, :], sh.stats[:, 0:tiles * 6]))

            def act_sqrt(out, v):
                dve.sem_inc(s["asked"], 1)
                dve.wait_ge(s["rooted"], 1)

            rsqrt_steps(nc, link, act_sqrt, scale[:, :], agg[:, 1:2], t1[:, :], t2[:, :], 1e-5)
            dve.wait_ge(s["gb_in"], 16)
            link(nc.vector.tensor_tensor(scale[:, :], scale[:, :], gb[:, 0:1], ALU.mult))
            link(nc.vector.tensor_tensor(t1[:, :], agg[:, 0:1], scale[:, :], ALU.mult))
            nc.vector.tensor_tensor(shift[:, :], gb[:, 1:2], t1[:, :], ALU.subtract).then_inc(s["ready"], 1)
            with dve.Fori(0, rounds) as g:
                for j in range(APPLY_RING):
                    n = g * APPLY_RING + j
                    dve.wait_ge(s["relu"], n + 1)
                    xt = sh.x[:, bass.ds(n * width, width)]
                    nc.vector.tensor_tensor(xt, xt, y[:, j, :], ALU.add).then_inc(s["added"], 1)
                    dve.wait_ge(s["added"], n + 1 + APPLY_RING)
                    for i in range(APPLY_T):
                        nc.vector.bn_stats(
                            sh.stats[:, bass.ds(n * (6 * APPLY_T) + 6 * i, 6)],
                            sh.x[:, bass.ds(n * width + i * TILE, TILE)]).then_inc(s["counted"], 1)


W_1, W_1B, W_B1, W_2, W_2S, W_B2, W_3R, W_3C, W_B3, W_END = (
    0, 32, 160, 161, 449, 737, 738, 866, 867, 868)

COPIES = ((-1, 1, None, 0), (-1, 1, 0), (-1, 0, 1))


def block_rows(i):
    return slice(32 * i, 32 * (i + 1))


def out_rows(i):
    return block_rows(3 - i)


def stack_stage(sh, tag, w_dram):
    nc = sh.nc
    groups = sh.images * TILES // BODY
    tiles = groups * BODY
    at = C_F1 + 2 * (sh.images * TILES // R1)
    first_flag, last_flag = (sh.const[:, at + i * groups:at + (i + 1) * groups] for i in range(2))
    a_rows = R2 * TR + 2
    z_rows = R2 * TR
    with ExitStack() as ctx:
        def sb(name, shape, dt=F32):
            return sh.sb(ctx, f"{tag}_{name}", shape, dt)

        m1_hi, m1_lo = sb("m1_hi", [P, P], F32R), sb("m1_lo", [P, P], F32R)
        m3_hi, m3_lo = sb("m3_hi", [P, P], F32R), sb("m3_lo", [P, P], F32R)
        u_hi, u_lo = sb("u_hi", [P, 9, P], F32R), sb("u_lo", [P, 9, P], F32R)
        v_hi, v_lo = ([sb(f"v_{n}{j}", [32 * len(COPIES[j]), 3, 32 * (3 - j)], F32R) for j in range(3)]
                      for n in ("hi", "lo"))
        c1, c3, b2 = sb("c1", [P, 1]), sb("c3", [P, 1]), sb("b2", [P, 1])
        scale, shift, scale1, shift3 = (sb(n, [P, groups]) for n in ("scale", "shift", "scale1", "shift3"))
        s = {n: sh.sem(f"{tag}_{n}") for n in (
            "w_in", "chain", "pe_chain", "zeroed", "xn", "xn_hi", "xn_lo", "s1", "a_hi", "a_lo", "mirrored",
            "s2", "s4", "s6", "s8", "sum0", "sum1", "sum2", "sum3", "z0_hi", "z1_hi", "z2_hi", "z0", "z1",
            "z2", "z0_lo", "z1_lo", "z2_lo", "r_hi", "r_lo", "f", "x_scaled", "updated", "counted")}

        with ExitStack() as prep:
            w = sh.sb(prep, f"{tag}_w", [P, W_END])
            d = sh.sb(prep, f"{tag}_d", [32, 4, P + 1])
            d0 = sh.sb(prep, f"{tag}_d0", [P, P])
            d1 = sh.sb(prep, f"{tag}_d1", [P, P])
            d2 = sh.sb(prep, f"{tag}_d2", [P, P])
            block = prep.enter_context(nc.Block())

            @block.sync
            def _(sp):
                sp.dma_start(w[:, :], w_dram).then_inc(s["w_in"], 16)

            @block.gpsimd
            def _(pool):
                for m in (u_hi, u_lo, *v_hi, *v_lo):
                    last = nc.gpsimd.memset(as_f32(m[tuple([slice(None)] * len(m.shape))]), 0.0)
                last.then_inc(s["zeroed"], 1)

            @block.tensor
            def _(pe):
                pe.wait_ge(s["w_in"], 16)
                nc.tensor.transpose(sh.bank[0][0:32, 0:P], w[:, W_1:W_1 + 32],
                                    sh.const[:, C_ID:C_ID + P]).then_inc(s["pe_chain"], 1)
                for i in range(3):
                    pe.wait_ge(s["chain"], 4 + 2 * i)
                    nc.tensor.matmul(sh.bank[1 + i][0:32, 0:P + 1], w[0:32, W_1B + 32 * i:W_1B + 32 * (i + 1)],
                                     d[:, i, :], start=True, stop=True).then_inc(s["pe_chain"], 1)
                pe.wait_ge(s["chain"], 10)
                for i in range(4):
                    last = nc.tensor.transpose(sh.bank[4][:, 32 * i:32 * (i + 1)], d[:, i, 0:P],
                                               sh.const[0:32, C_ID:C_ID + 32])
                last.then_inc(s["pe_chain"], 1)

            @block.vector
            def _(dve):
                link = Chain(dve, s["chain"])
                group_tables(nc, sh, link, TILES // BODY, scale, shift)
                dve.wait_ge(s["w_in"], 16)
                dve.wait_ge(s["pe_chain"], 1)
                link(nc.vector.tensor_copy(d[:, 0, 0:P], sh.bank[0][0:32, 0:P]))
                link(nc.vector.tensor_copy(d[:, 0, P:P + 1], w[0:32, W_B1:W_B1 + 1]))
                for i in range(3):
                    dve.wait_ge(s["pe_chain"], 2 + i)
                    link(nc.vector.tensor_tensor(d[:, i + 1, :], d[:, i, :], sh.bank[1 + i][0:32, 0:P + 1], ALU.add))
                    own = slice(32 * i, 32 * (i + 1))
                    link(nc.vector.tensor_tensor(d[:, i + 1, own], d[:, i + 1, own], d[:, 0, own], ALU.subtract))
                for i in range(4):
                    link(nc.vector.tensor_copy(c1[32 * i:32 * (i + 1), :], d[:, i, P:P + 1]))
                dve.wait_ge(s["pe_chain"], 5)
                link(nc.vector.tensor_copy(m1_hi[:, :], sh.bank[4][:, 0:P]))
                link(nc.vector.tensor_tensor(m1_lo[:, :], sh.bank[4][:, 0:P], as_f32(m1_hi[:, :]), ALU.subtract))
                w3 = w[:, W_3R:W_3R + P - 1]
                link(nc.vector.memset(d0[:, 0:1], 1.0))
                link(nc.vector.tensor_scalar(d0[:, 1:P], w3, 1.0, None, ALU.add))
                link(nc.vector.memset(d1[:, 0:1], 0.0))
                link(nc.vector.scalar_tensor_tensor(d1[:, 1:P], w3, -1.0, sh.const[:, C_ID:C_ID + P - 1],
                                                    ALU.mult, ALU.mult))
                link(nc.vector.tensor_tensor_scan(d2[:, :], d0[:, :], d1[:, :], w[:, W_3C:W_3C + 1],
                                                  ALU.mult, ALU.add))
                for i in range(4):
                    link(nc.vector.tensor_copy(d1[out_rows(i), :], d2[block_rows(i), :]))
                link(nc.vector.tensor_copy(m3_hi[:, :], d1[:, :]))
                link(nc.vector.tensor_tensor(m3_lo[:, :], d1[:, :], as_f32(m3_hi[:, :]), ALU.subtract))
                link(nc.vector.memset(d1[:, :], 0.0))
                link(nc.vector.tensor_tensor_scan(d2[:, :], d0[:, :], d1[:, :], w[:, W_B3:W_B3 + 1],
                                                  ALU.mult, ALU.add))
                link(nc.vector.tensor_tensor(d2[:, :], d2[:, :], sh.const[:, C_ID:C_ID + P], ALU.mult))
                link(nc.vector.reduce_sum(c3[:, :], d2[:, :], AX.X))
                link(nc.vector.tensor_scalar(scale1[:, :], scale[:, :], 1.0, None, ALU.add))
                link(nc.vector.tensor_scalar(shift3[:, :], shift[:, :], c3[:, 0:1], None, ALU.add))
                link(nc.vector.tensor_copy(b2[:, :], w[:, W_B2:W_B2 + 1]))
                dve.wait_ge(s["zeroed"], 1)
                for q in range(4):
                    rows = block_rows(q)
                    src = w[rows, W_2:W_2 + 288].rearrange("p (t e) -> p t e", e=32)
                    for i in range(q + 1):
                        to = (rows, slice(None), out_rows(i))
                        link(nc.vector.tensor_copy(u_hi[to], src))
                        link(nc.vector.tensor_tensor(u_lo[to], src, as_f32(u_hi[:, :, :])[to], ALU.subtract))
                for j in range(3):
                    rows = slice(0, 32 * len(COPIES[j]))
                    src = w[rows, W_2S + 96 * j:W_2S + 96 * (j + 1)].rearrange("p (x e) -> p x e", e=32)
                    for i in range(j + 1, 4):
                        to = (rows, slice(None), out_rows(i))
                        link(nc.vector.tensor_copy(v_hi[j][to], src))
                        link(nc.vector.tensor_tensor(v_lo[j][to], src, as_f32(v_hi[j][:, :, :])[to],
                                                     ALU.subtract))

        xn = sb("xn", [P, TILE])
        xn_hi = [sb(f"xn_hi{i}", [P, TILE], F32R) for i in range(2)]
        xn_lo = [sb(f"xn_lo{i}", [P, TILE], F32R) for i in range(2)]
        a_f = sb("a_f", [P, TILE])
        a_hi, a_lo = (sb(n, [P, a_rows, PITCH], F32R) for n in ("ring_a_hi", "ring_a_lo"))
        acc = sb("acc", [P, BODY, TILE])
        z = [sb(f"ring_z{i}", [32 * len(COPIES[i]), 2, z_rows, PITCH], F32R) for i in range(3)]
        r_hi, r_lo = sb("r_hi", [P, TILE], F32R), sb("r_lo", [P, TILE], F32R)
        ps_d, ps_z, ps_a, ps_f = sh.bank[0:2], sh.bank[2:5], sh.bank[6], sh.bank[7]
        inner = slice(1, 1 + SIDE)

        def grid(ap):
            return ap.rearrange("p (r c) -> p r c", c=SIDE)

        def valid(t):
            return not isinstance(t, int) or 0 <= t < tiles

        def upto(t):
            return min(t, tiles) if isinstance(t, int) else t

        def group_of(g, j, lag):
            return g + (j - lag) // BODY

        def walk(eng, step):
            for t in range(-3, BODY):
                step(t // BODY, t % BODY, t)
            with eng.Fori(1, groups - 1) as g:
                for j in range(BODY):
                    step(g, j, g * BODY + j)
            for t in range(tiles - BODY, tiles + 5):
                step(t // BODY, t % BODY, t)

        block = ctx.enter_context(nc.Block())

        @block.gpsimd
        def _(pool):
            nc.gpsimd.memset(as_f32(a_hi[:, :, :]), 0.0)
            nc.gpsimd.memset(as_f32(a_lo[:, :, :]), 0.0)
            for i in range(3):
                last = nc.gpsimd.memset(as_f32(z[i][:, :, :, :]), 0.0)
            last.then_inc(s["mirrored"], 1)

            def step(g, j, k):
                t, i = k + 3, (j + 3) % 2
                if valid(t):
                    pool.wait_ge(s["xn"], t + 1)
                    pool.wait_ge(s["xn_hi"], t + 1)
                    wait(pool, s["s1"], t - 1)
                    nc.gpsimd.tensor_tensor(xn_lo[i][:, :], xn[:, :], as_f32(xn_hi[i][:, :]),
                                            ALU.subtract).then_inc(s["xn_lo"], 1)
                t, jt = k + 2, (j + 2) % BODY
                if valid(t) and jt % R2 != 1:
                    src, dst = (1, a_rows - 1) if jt % R2 == 0 else (R2 * TR, 0)
                    gt = group_of(g, j, -2)
                    flag = {0: first_flag[:, bass.ds(gt, 1)], BODY - 1: last_flag[:, bass.ds(gt, 1)]}.get(
                        jt, sh.const[:, C_ONE:C_ONE + 1])
                    pool.wait_ge(s["a_hi"], t + 1)
                    pool.wait_ge(s["a_lo"], t + 1)
                    for ring in (a_hi, a_lo):
                        last = nc.gpsimd.tensor_tensor(ring[:, dst, :], as_f32(ring[:, src, :]),
                                                       flag.broadcast_to([P, PITCH]), ALU.mult)
                    last.then_inc(s["mirrored"], 1)
                if isinstance(t, int) and t == tiles:
                    pool.wait_ge(s["s2"], tiles - R2)
                    nc.gpsimd.memset(as_f32(a_hi[:, a_rows - 1, :]), 0.0)
                    nc.gpsimd.memset(as_f32(a_lo[:, a_rows - 1, :]), 0.0).then_inc(s["mirrored"], 1)

            walk(pool, step)

        @block.scalar
        def _(act):
            act.wait_ge(s["mirrored"], 1)

            def high_z(i, t, jt):
                if valid(t):
                    act.wait_ge(s[f"sum{i}"], t + 1)
                    r0, own = TR * (jt % R2), out_rows(i)
                    nc.scalar.activation(z[i][own, 0, r0:r0 + TR, inner], grid(acc[own, jt, :]),
                                         ACT.Copy).then_inc(s[f"z{i}_hi"], 1)

            def step(g, j, k):
                t, i = k + 3, (j + 3) % 2
                if valid(t):
                    gt = group_of(g, j, -3)
                    wait(act, s["s1"], t - 1)
                    wait(act, s["xn_lo"], t)
                    nc.scalar.activation(xn_hi[i][:, :], sh.x[:, bass.ds(t * TILE, TILE)], ACT.Identity,
                                         scale=scale[:, bass.ds(gt, 1)],
                                         bias=shift[:, bass.ds(gt, 1)]).then_inc(s["xn_hi"], 1)
                    nc.scalar.activation(xn[:, :], sh.x[:, bass.ds(t * TILE, TILE)], ACT.Identity,
                                         scale=scale[:, bass.ds(gt, 1)],
                                         bias=shift[:, bass.ds(gt, 1)]).then_inc(s["xn"], 1)
                t, jt = k + 2, (j + 2) % BODY
                if valid(t):
                    act.wait_ge(s["s1"], t + 1)
                    r0 = 1 + TR * (jt % R2)
                    nc.scalar.activation(a_hi[:, r0:r0 + TR, inner], grid(ps_a[:, 0:TILE]), ACT.Relu,
                                         bias=c1[:, 0:1])
                    wait(act, s["a_lo"], t)
                    nc.scalar.activation(a_f[:, :], ps_a[:, 0:TILE], ACT.Relu,
                                         bias=c1[:, 0:1]).then_inc(s["a_hi"], 1)
                high_z(1, k - 2, (j - 2) % BODY)
                t, jt = k - 5, (j - 5) % BODY
                if valid(t):
                    act.wait_ge(s["sum3"], t + 1)
                    wait(act, s["f"], t)
                    nc.scalar.activation(r_hi[:, :], acc[:, jt, :], ACT.Relu).then_inc(s["r_hi"], 1)
                    gt = group_of(g, j, 5)
                    xt = sh.x[:, bass.ds(t * TILE, TILE)]
                    nc.scalar.activation(xt, xt, ACT.Identity, scale=scale1[:, bass.ds(gt, 1)],
                                         bias=shift3[:, bass.ds(gt, 1)]).then_inc(s["x_scaled"], 1)
                if valid(k):
                    act.wait_ge(s["s2"], k + 1)
                    nc.scalar.activation(acc[:, j, :], ps_d[j % 2][:, 0:TILE], ACT.Identity,
                                         bias=b2[:, 0:1]).then_inc(s["sum0"], 1)
                    high_z(0, k, j)
                high_z(2, k - 3, (j - 3) % BODY)

            walk(act, step)

        @block.vector
        def _(dve):
            dve.wait_ge(s["mirrored"], 1)

            def add_up(i, t, jt):
                if valid(t):
                    dve.wait_ge(s[("s4", "s6", "s8")[i - 1]], t + 1)
                    dve.wait_ge(s[f"sum{i - 1}"], t + 1)
                    rows = slice(0, 32 * (4 - i))
                    nc.vector.tensor_tensor(acc[rows, jt, :], acc[rows, jt, :], ps_z[i - 1][rows, 0:TILE],
                                            ALU.add).then_inc(s[f"sum{i}"], 1)

            def shift_z(i, g, j, lag):
                t, jt = g * BODY + (j - lag), (j - lag) % BODY
                gt = group_of(g, j, lag)
                if not valid(t):
                    return
                zi, slot = z[i], jt % R2
                r0 = TR * slot
                own, down, up = (block_rows(COPIES[i].index(dy)) for dy in (0, -1, 1))
                dve.wait_ge(s[f"z{i}_hi"], t + 1)
                nc.vector.tensor_tensor(zi[own, 1, r0:r0 + TR, inner], grid(acc[own, jt, :]),
                                        as_f32(zi[own, 0, r0:r0 + TR, inner]), ALU.subtract)\
                    .then_inc(s[f"z{i}_lo"], 1)
                dve.wait_ge(s[f"z{i}_lo"], t + 1)
                mid = as_f32(zi[own, :, :, :])
                n0 = TR if slot < R2 - 1 else TR - 1
                nc.vector.tensor_copy(zi[down, :, r0 + 1:r0 + 1 + n0, inner], mid[:, :, r0:r0 + n0, inner])
                f2 = 0 if slot else 1
                last = nc.vector.tensor_copy(zi[up, :, r0 - 1 + f2:r0 - 1 + TR, inner],
                                             mid[:, :, r0 + f2:r0 + TR, inner])
                if slot == R2 - 1:
                    flag = last_flag[own, bass.ds(gt, 1)] if jt == BODY - 1 else 1.0
                    last = nc.vector.tensor_scalar(zi[down, :, 0, inner], mid[:, :, z_rows - 1, inner],
                                                   flag, None, ALU.mult)
                if slot == 0:
                    flag = first_flag[own, bass.ds(gt, 1)] if jt == 0 else 1.0
                    last = nc.vector.tensor_scalar(zi[up, :, z_rows - 1, inner], mid[:, :, 0, inner],
                                                   flag, None, ALU.mult)
                last.then_inc(s[f"z{i}"], 1)
                if isinstance(t, int) and t == tiles - 1:
                    dve.wait_ge(s[("s4", "s6", "s8")[i]], tiles - R2)
                    nc.vector.memset(as_f32(zi[up, :, z_rows - 1, inner]), 0.0).then_inc(s[f"z{i}"], 1)

            def step(g, j, k):
                t, jt = k + 2, (j + 2) % BODY
                if valid(t):
                    dve.wait_ge(s["a_hi"], t + 1)
                    r0 = 1 + TR * (jt % R2)
                    nc.vector.tensor_tensor(a_lo[:, r0:r0 + TR, inner], grid(a_f[:, :]),
                                            as_f32(a_hi[:, r0:r0 + TR, inner]), ALU.subtract)\
                        .then_inc(s["a_lo"], 1)
                add_up(1, k - 2, (j - 2) % BODY)
                shift_z(1, g, j, 2)
                t, jt = k - 5, (j - 5) % BODY
                add_up(3, t, jt)
                if valid(t):
                    dve.wait_ge(s["r_hi"], t + 1)
                    nc.vector.scalar_tensor_tensor(r_lo[:, :], acc[:, jt, :], 0.0, as_f32(r_hi[:, :]),
                                                   ALU.max, ALU.subtract).then_inc(s["r_lo"], 1)
                shift_z(0, g, j, 0)
                add_up(2, k - 3, (j - 3) % BODY)
                shift_z(2, g, j, 3)
                t = k - 5
                if valid(t):
                    dve.wait_ge(s["f"], t + 1)
                    dve.wait_ge(s["x_scaled"], t + 1)
                    xt = sh.x[:, bass.ds(t * TILE, TILE)]
                    nc.vector.tensor_tensor(xt, xt, ps_f[:, 0:TILE], ALU.add).then_inc(s["updated"], 1)
                    dve.wait_ge(s["updated"], t + 1)
                    nc.vector.bn_stats(sh.stats[:, bass.ds(t * 6, 6)], xt).then_inc(s["counted"], 1)

            walk(dve, step)

        @block.tensor
        def _(pe):
            def dense(g, j, k, part):
                if not valid(k):
                    return
                if part == 0:
                    pe.wait_ge(s["a_hi"], upto(k + 2))
                    pe.wait_ge(s["a_lo"], upto(k + 2))
                    mirrored_for(g, j)
                    wait(pe, s["sum0"], k - 1)
                out = grid(ps_d[j % 2][:, 0:TILE])
                r0 = 1 + TR * (j % R2)
                for n, (dy, dx) in list(enumerate(TAPS))[:5] if part == 0 else list(enumerate(TAPS))[5:]:
                    rows, cols = slice(r0 + dy, r0 + dy + TR), slice(1 + dx, 1 + dx + SIDE)
                    last = split_product(nc, out, u_hi[:, n, :], u_lo[:, n, :], a_hi[:, rows, cols],
                                         a_lo[:, rows, cols], start=n == 0, stop=n == 8)
                if part:
                    last.then_inc(s["s2"], 1)

            def mirrored_for(g, j):
                if j % R2 == 0:
                    pe.wait_ge(s["mirrored"], g * 4 + (j // R2) * 2 + 1)
                if j % R2 == R2 - 1:
                    pe.wait_ge(s["mirrored"], g * 4 + (j // R2) * 2 + 4)

            def add_block(i, t, jt, done):
                if not valid(t):
                    return
                extra = 1 if isinstance(t, int) and t == tiles - 1 else 0
                pe.wait_ge(s[f"z{i}"], upto(t + 2) + extra)
                wait(pe, s[f"sum{i + 1}"], t)
                out = grid(ps_z[i][0:32 * (3 - i), 0:TILE])
                r0 = TR * (jt % R2)
                for dx in range(3):
                    zi = (z[i][:, half, r0:r0 + TR, dx:dx + SIDE] for half in range(2))
                    last = split_product(nc, out, v_hi[i][:, dx, :], v_lo[i][:, dx, :], *zi,
                                         start=dx == 0, stop=dx == 2)
                last.then_inc(s[done], 1)

            def step(g, j, k):
                dense(g, j, k, 0)
                t, i = k + 2, (j + 2) % 2
                if valid(t):
                    pe.wait_ge(s["xn_hi"], t + 1)
                    pe.wait_ge(s["xn_lo"], t + 1)
                    wait(pe, s["a_hi"], t)
                    split_product(nc, ps_a[:, 0:TILE], m1_hi[:, :], m1_lo[:, :], xn_hi[i][:, :],
                                  xn_lo[i][:, :]).then_inc(s["s1"], 1)
                add_block(0, k - 2, (j - 2) % BODY, "s4")
                add_block(2, k - 5, (j - 5) % BODY, "s8")
                dense(g, j, k, 1)
                add_block(1, k - 3, (j - 3) % BODY, "s6")
                t = k - 5
                if valid(t):
                    pe.wait_ge(s["r_hi"], t + 1)
                    pe.wait_ge(s["r_lo"], t + 1)
                    wait(pe, s["updated"], t)
                    split_product(nc, ps_f[:, 0:TILE], m3_hi[:, :], m3_lo[:, :], r_hi[:, :],
                                  r_lo[:, :]).then_inc(s["f"], 1)

            walk(pe, step)


def store_stage(sh, out_dram):
    nc = sh.nc
    rounds = sh.tokens // (CHUNKS * BANK)
    with ExitStack() as ctx:
        buf = sh.sb(ctx, "store_buf", [P, CHUNKS, 4, P])
        turned, kept = sh.sem("store_turned"), sh.sem("store_kept")
        stored = [sh.sem(f"stored{i}") for i in range(CHUNKS)]
        out_v = out_dram.rearrange("(g i t p) c -> p i t g c", i=CHUNKS, t=4, p=P)
        block = ctx.enter_context(nc.Block())

        @block.tensor
        def _(pe):
            for g in range(rounds):
                for n in range(CHUNKS):
                    pe.wait_ge(kept, g * CHUNKS + n + 1)
                    for t in range(4):
                        at = (g * CHUNKS + n) * BANK + t * P
                        last = nc.tensor.transpose(
                            sh.bank[n][:, t * P:(t + 1) * P], sh.x[:, at:at + P],
                            sh.const[:, C_ID:C_ID + P])
                    last.then_inc(turned, 1)

        @block.scalar
        def _(act):
            act.sem_inc(kept, CHUNKS)
            with act.Fori(0, rounds) as g:
                for n in range(CHUNKS):
                    act.wait_ge(turned, g * CHUNKS + n + 1)
                    act.wait_ge(stored[n], g * 16 + 16)
                    nc.scalar.activation(buf[:, n].rearrange("p t c -> p (t c)"), sh.bank[n][:, :],
                                         ACT.Copy).then_inc(kept, 1)

        @block.sync
        def _(sp):
            for n in range(CHUNKS):
                sp.sem_inc(stored[n], 16)
            with sp.Fori(0, rounds) as g:
                for n in range(CHUNKS):
                    sp.wait_ge(kept, g * CHUNKS + n + 1 + CHUNKS)
                    sp.dma_start(out_v[:, n, :, bass.ds(g, 1), :].rearrange("p t g c -> p (t g) c"), buf[:, n])\
                        .then_inc(stored[n], 16)
            for n in range(CHUNKS):
                sp.wait_ge(stored[n], 16 * (rounds + 1))


def program(nc, x, const, at_w, at_b, at_tables, c1_w, c1_b, bn, w2, w3, out):
    images = x.shape[0] // IMG
    with ExitStack() as ctx:
        sh = Shared(nc, ctx, images)
        y = nc.dram_tensor("y", [P, sh.tokens], F32, kind="Internal").ap()
        load_stage(sh, x, const)
        group_norm_stage(sh, "gn0", IMG // BANK)
        attention_stage(sh, at_w, at_b, at_tables)
        sh.recycle()
        group_norm_stage(sh, "gn1", TILES)
        conv1_stage(sh, c1_w, c1_b, y)
        batch_norm_stage(sh, bn, y)
        group_norm_stage(sh, "gn2", TILES)
        stack_stage(sh, "l2", w2)
        group_norm_stage(sh, "gn3", TILES)
        stack_stage(sh, "l3", w3)
        store_stage(sh, out)


def stacked_taps(w2):
    w2 = w2.reshape(3, 3, 4, 32, 32)
    out = np.zeros((3, 4, 32, 3, 32), np.float32)
    for i in range(3):
        for group, dy in enumerate(COPIES[i]):
            if dy is not None:
                out[i, group] = w2[1 + dy, :, i].transpose(1, 0, 2)
    return out.transpose(1, 2, 0, 3, 4).reshape(P, 288)


def pack_stack(w1, b1, w2, b2, w3, b3):
    out = np.zeros((P, W_END), np.float32)
    w1, w2, w3 = w1.reshape(P, 32), w2.reshape(3, 3, P, 32), w3.reshape(P)
    out[:, W_1:W_1B] = w1
    out[:32, W_1B:W_B1] = w1.reshape(4, 32, 32).transpose(1, 0, 2).reshape(32, P)
    out[:32, W_B1] = b1.reshape(32)
    out[:, W_2:W_2S] = w2.transpose(2, 0, 1, 3).reshape(P, 288)
    out[:, W_2S:W_B2] = stacked_taps(w2)
    out[:, W_B2] = np.tile(b2.reshape(32), 4)
    out[:, W_3R:W_3C] = w3[None]
    out[:, W_3C] = w3
    out[:, W_B3] = b3.reshape(1)
    return out


def kernel(**inputs):
    import concourse.bacc as bacc
    from concourse.bass_utils import run_bass_kernel_spmd

    x = np.asarray(inputs["x"])
    images = x.shape[0]
    wq, bq = np.asarray(inputs["L0_conv_W_qkv"]), np.asarray(inputs["L0_conv_b_qkv"])
    c = np.arange(P)
    partner = c + np.where(c % 8 < 4, 4, -4)
    even_odd = np.argsort(c // HD % 2, kind="stable")
    w = [wq[:, :P], wq[:, :P][:, partner], wq[:, P:2 * P], wq[:, P:2 * P][:, partner],
         wq[:, 2 * P:][:, even_odd], np.asarray(inputs["L0_conv_W_proj"])]
    b = [bq[:P], bq[:P][partner], bq[P:2 * P], bq[P:2 * P][partner], bq[2 * P:],
         np.asarray(inputs["L0_conv_b_proj"])]
    arrays = {
        "x": x.reshape(-1, P),
        "const": constants(images),
        "at_w": np.concatenate(w, 1),
        "at_b": np.stack(b, 1),
        "at_tables": attention_tables(),
        "c1_w": np.asarray(inputs["L1_conv_w"]).reshape(9, 4, P)[:, c % 4].transpose(1, 0, 2),
        "c1_b": np.asarray(inputs["L1_conv_b"])[:, None],
        "bn": np.stack([np.asarray(inputs[f"L1_conv_{n}"]) for n in ("gamma", "beta")], 1),
        "w2": pack_stack(*(np.asarray(inputs[f"L2_conv_{n}"]) for n in ("w1", "b1", "w2", "b2", "w3", "b3"))),
        "w3": pack_stack(*(np.asarray(inputs[f"L3_conv_{n}"]) for n in ("w1", "b1", "w2", "b2", "w3", "b3"))),
    }
    arrays = {f"in_{k}": np.ascontiguousarray(v) for k, v in arrays.items()}
    nc = bacc.Bacc("TRN2", target_bir_lowering=False, num_devices=1, dynamic_dma_scratch_size=1024)
    args = [nc.dram_tensor(k, v.shape, F32, kind="ExternalInput").ap() for k, v in arrays.items()]
    args.append(nc.dram_tensor("out", arrays["in_x"].shape, F32, kind="ExternalOutput").ap())
    program(nc, *args)
    r = run_bass_kernel_spmd(nc, [arrays], core_ids=[0])
    return r.results[0]["out"].reshape(x.shape)
```

```python
from contextlib import ExitStack

import numpy as np

import concourse.bass as bass
from concourse import mybir

F32 = mybir.dt.float32
F32R = mybir.dt.float32r
ALU = mybir.AluOpType
ACT = mybir.ActivationFunctionType
AX = mybir.AxisListType

P = 128
SIDE = 96
IMG = SIDE * SIDE
BANK = 512

HEADS, HD, WIN = 8, 16, 64
QUAD = 4 * WIN
ROW_STEPS = SIDE // 16
STEPS = ROW_STEPS * ROW_STEPS
ROLL = 4
FAR = 3.0e38

TR = 4
TILE = TR * SIDE
TILES = IMG // TILE
PITCH = SIDE + 2
R1 = 4
R2 = 3
BODY = 6

C_ID, C_GAVG = 0, 128
C_ONE, C_F1 = 256, 257
T_CQ, T_SQ, T_CK, T_SK, T_LIM, T_END = 0, 64, 128, 192, 256, 320


def n_flags(images):
    return images * TILES // R1, images * TILES // BODY


def constants(images):
    c = np.arange(P)
    n1, n2 = n_flags(images)
    out = np.zeros((P, C_F1 + 2 * n1 + 2 * n2), np.float32)
    out[:, C_ID:C_ID + P] = np.eye(P)
    out[:, C_GAVG:C_GAVG + P] = (c[:, None] // 4 == c[None] // 4) * 0.25
    out[:, C_ONE] = 1.0
    at = C_F1
    for count, tiles in ((n1, R1), (n2, BODY)):
        g = np.arange(count)
        out[:, at:at + count] = g * tiles % TILES != 0
        out[:, at + count:at + 2 * count] = (g + 1) * tiles % TILES != 0
        at += 2 * count
    return out


def attention_tables():
    out = np.zeros((P, T_END), np.float32)
    inv = (1.0 / 10000.0 ** (np.arange(4, dtype=np.float32) / 4)).astype(np.float32)
    c = np.arange(P)
    d = c % HD
    n = np.arange(WIN)
    pos = np.where((d < 8)[:, None], (n // 8)[None], (n % 8)[None]).astype(np.float32)
    ang = (pos * inv[d % 4][:, None]).astype(np.float32)
    sign = np.where(d % 8 < 4, -1.0, 1.0)[:, None]
    cos, sin = np.cos(ang), np.sin(ang) * sign
    out[:, T_CQ:T_CQ + WIN], out[:, T_SQ:T_SQ + WIN] = cos * HD ** -0.5, sin * HD ** -0.5
    out[:, T_CK:T_CK + WIN], out[:, T_SK:T_SK + WIN] = cos, sin
    region = np.array([0, 0, 0, 0, 1, 1, 2, 2])[n // 8]
    out[:, T_LIM:T_LIM + WIN] = np.where(region[c % WIN][:, None] == region[None], FAR, -FAR)
    return out


def wait(eng, sem, n):
    if not isinstance(n, int) or n > 0:
        eng.wait_ge(sem, n)


class Chain:

    def __init__(self, eng, sem):
        self.eng, self.sem, self.n = eng, sem, 0

    def __call__(self, ins):
        self.n += 1
        ins.then_inc(self.sem, 1)
        self.eng.wait_ge(self.sem, self.n)


class Shared:

    def __init__(self, nc, ctx, images):
        self.nc, self.ctx, self.images = nc, ctx, images
        self.tokens = images * IMG
        self.sems = []
        n1, n2 = n_flags(images)
        self.x = self.sb(ctx, "x_res", [P, self.tokens])
        self.const = self.sb(ctx, "const", [P, C_F1 + 2 * n1 + 2 * n2])
        self.stats = self.sb(ctx, "stats", [P, max(images * TILES * 6, TILE)])
        self.gscale = self.sb(ctx, "gscale", [P, images])
        self.gshift = self.sb(ctx, "gshift", [P, images])
        self.bank = [ctx.enter_context(nc.psum_tensor(f"bank{i}", [P, BANK], F32)) for i in range(8)]

    def sb(self, ctx, name, shape, dt=F32):
        return ctx.enter_context(self.nc.sbuf_tensor(name, shape, dt))

    def sem(self, name):
        self.sems.append(self.nc.alloc_semaphore(name=name))
        return self.sems[-1]

    def recycle(self):
        self.nc.clear_and_free_semaphores(self.sems)
        self.nc.all_engine_barrier()
        self.sems = []


def is_prologue(q):
    return isinstance(q, int) and q < 2


def split_product(nc, out, w_hi, w_lo, x_hi, x_lo, start=True, stop=True):
    nc.tensor.matmul(out, w_hi, x_hi, start=start, stop=False)
    nc.tensor.matmul(out, w_hi, x_lo, start=False, stop=False)
    return nc.tensor.matmul(out, w_lo, x_hi, start=False, stop=stop)


def as_f32(ap):
    return ap.bitcast(F32)


LOAD_T = 8
LOAD_RING = 3
CHUNKS = 2 * LOAD_RING


def load_stage(sh, x_dram, const_dram):
    nc = sh.nc
    rounds = sh.tokens // (LOAD_RING * LOAD_T * P)
    with ExitStack() as ctx:
        raw = sh.sb(ctx, "load_raw", [P, LOAD_RING, LOAD_T, P])
        const_in = sh.sem("load_const_in")
        raw_in = [sh.sem(f"load_raw_in{i}") for i in range(LOAD_RING)]
        turned, kept, counted = sh.sem("load_turned"), sh.sem("load_kept"), sh.sem("load_counted")
        x_v = x_dram.rearrange("(g i t p) c -> p i t g c", i=LOAD_RING, t=LOAD_T, p=P)
        block = ctx.enter_context(nc.Block())

        @block.sync
        def _(sp):
            sp.dma_start(sh.const[:, :], const_dram).then_inc(const_in, 16)
            with sp.Fori(0, rounds) as g:
                for i in range(LOAD_RING):
                    sp.wait_ge(turned, g * CHUNKS + 2 * i + 2)
                    sp.dma_start(raw[:, i], x_v[:, i, :, bass.ds(g, 1), :].rearrange("p t g c -> p (t g) c"))\
                        .then_inc(raw_in[i], 16)

        @block.tensor
        def _(pe):
            pe.sem_inc(turned, CHUNKS)
            pe.wait_ge(const_in, 16)
            with pe.Fori(0, rounds) as g:
                for n in range(CHUNKS):
                    i, half = n // 2, n % 2
                    if half == 0:
                        pe.wait_ge(raw_in[i], g * 16 + 16)
                    pe.wait_ge(kept, g * CHUNKS + n + 1)
                    for t in range(4):
                        last = nc.tensor.transpose(
                            sh.bank[n][:, t * P:(t + 1) * P], raw[:, i, 4 * half + t, :],
                            sh.const[:, C_ID:C_ID + P])
                    last.then_inc(turned, 1)

        @block.scalar
        def _(act):
            act.sem_inc(kept, CHUNKS)
            with act.Fori(0, rounds) as g:
                for n in range(CHUNKS):
                    chunk = g * CHUNKS + n
                    act.wait_ge(turned, chunk + 1 + CHUNKS)
                    nc.scalar.activation(sh.x[:, bass.ds(chunk * BANK, BANK)], sh.bank[n][:, :],
                                         ACT.Copy).then_inc(kept, 1)

        @block.vector
        def _(dve):
            with dve.Fori(0, rounds) as g:
                for n in range(CHUNKS):
                    chunk = g * CHUNKS + n
                    dve.wait_ge(kept, chunk + 1 + CHUNKS)
                    nc.vector.bn_stats(sh.stats[:, bass.ds(chunk * 6, 6)],
                                       sh.x[:, bass.ds(chunk * BANK, BANK)]).then_inc(counted, 1)


def rsqrt_steps(nc, link, act_sqrt, out, v, t1, t2, eps):
    link(nc.vector.tensor_scalar(t1, v, eps, None, ALU.add))
    act_sqrt(t2, t1)
    link(nc.vector.reciprocal(out, t2))
    link(nc.vector.tensor_tensor(t2, out, out, ALU.mult))
    link(nc.vector.tensor_tensor(t2, t2, t1, ALU.mult))
    link(nc.vector.tensor_scalar(t2, t2, -0.5, 1.5, ALU.mult, ALU.add))
    link(nc.vector.tensor_tensor(out, out, t2, ALU.mult))


def group_norm_stage(sh, tag, chunks):
    nc, B = sh.nc, sh.images
    with ExitStack() as ctx:
        agg = sh.sb(ctx, f"{tag}_agg", [P, B, 2])
        t1, t2, t3 = (sh.sb(ctx, f"{tag}_t{i}", [P, B]) for i in range(3))
        chain, asked, rooted = sh.sem(f"{tag}_chain"), sh.sem(f"{tag}_asked"), sh.sem(f"{tag}_rooted")
        averaged, to_average = sh.sem(f"{tag}_averaged"), sh.sem(f"{tag}_to_average")
        mean_ps, var_ps = sh.bank[0][:, 0:B], sh.bank[1][:, 0:B]
        gavg = sh.const[:, C_GAVG:C_GAVG + P]
        block = ctx.enter_context(nc.Block())

        @block.tensor
        def _(pe):
            pe.wait_ge(to_average, 1)
            nc.tensor.matmul(mean_ps, gavg, t3[:, :], start=True, stop=True).then_inc(averaged, 1)
            pe.wait_ge(to_average, 2)
            nc.tensor.matmul(var_ps, gavg, t2[:, :], start=True, stop=True).then_inc(averaged, 1)

        @block.scalar
        def _(act):
            act.wait_ge(asked, 1)
            nc.scalar.activation(t2[:, :], t1[:, :], ACT.Sqrt).then_inc(rooted, 1)

        @block.vector
        def _(dve):
            link = Chain(dve, chain)
            for b in range(B):
                link(nc.vector.bn_aggr(agg[:, b, :], sh.stats[:, b * chunks * 6:(b + 1) * chunks * 6]))
            nc.vector.tensor_copy(t3[:, :], agg[:, :, 0]).then_inc(to_average, 1)
            dve.wait_ge(averaged, 1)
            link(nc.vector.tensor_copy(sh.gshift[:, 0:B], mean_ps))
            link(nc.vector.tensor_tensor(t1[:, :], t3[:, :], sh.gshift[:, 0:B], ALU.subtract))
            link(nc.vector.tensor_tensor(t1[:, :], t1[:, :], t1[:, :], ALU.mult))
            nc.vector.tensor_tensor(t2[:, :], t1[:, :], agg[:, :, 1], ALU.add).then_inc(to_average, 1)
            dve.wait_ge(averaged, 2)

            def act_sqrt(out, v):
                dve.sem_inc(asked, 1)
                dve.wait_ge(rooted, 1)

            rsqrt_steps(nc, link, act_sqrt, sh.gscale[:, 0:B], var_ps, t1[:, :], t2[:, :], 1e-5)
            link(nc.vector.scalar_tensor_tensor(sh.gshift[:, 0:B], sh.gshift[:, 0:B], -1.0,
                                                sh.gscale[:, 0:B], ALU.mult, ALU.mult))


class BlockRow:

    def __init__(self, b, r, half):
        self.b, self.r, self.half = b, r, half
        self.number = b * ROW_STEPS + r
        self.masked = isinstance(r, int) and r == ROW_STEPS - 1
        self.first = isinstance(b, int) and isinstance(r, int) and b == r == 0

    def starts(self, j):
        return self.first and j == 0

    def ahead(self, j):
        n = self.number * ROW_STEPS + j
        if not (self.masked and j >= ROW_STEPS - 3):
            return self.b, n * QUAD + 3 * QUAD
        if isinstance(self.b, int):
            return 0, (n + 3) % STEPS * QUAD
        return self.b + 1, n * QUAD + 3 * QUAD

    def tile_before(self, i):
        if isinstance(self.r, int) and self.r == 0:
            return (self.b - 1) * TILES + ((ROW_STEPS - 1) * 4 + 1 + i) % TILES
        return self.b * TILES + (self.r - 1) * 4 + 1 + i


def attention_stage(sh, w_dram, b_dram, tables_dram):
    nc, B = sh.nc, sh.images
    with ExitStack() as ctx:
        w = sh.sb(ctx, "at_w", [P, 6 * P])
        w_hi = sh.sb(ctx, "at_w_hi", [P, 4 * P], F32R)
        w_lo = sh.sb(ctx, "at_w_lo", [P, 4 * P], F32R)
        tables = sh.sb(ctx, "at_tables", [P, T_END])
        bias = sh.sb(ctx, "at_bias", [P, 6])
        b_out = sh.sb(ctx, "at_b_out", [P, 1])
        w_v, w_p = w[:, 4 * P:5 * P], w[:, 5 * P:6 * P]
        xn = [sh.sb(ctx, f"at_xn{i}", [P, QUAD]) for i in range(2)]
        xn_hi = [sh.sb(ctx, f"at_xn_hi{i}", [P, QUAD], F32R) for i in range(2)]
        xn_lo = [sh.sb(ctx, f"at_xn_lo{i}", [P, QUAD], F32R) for i in range(2)]
        turn = [sh.sb(ctx, f"at_turn{i}", [P, QUAD]) for i in range(4)]
        q_r = [sh.sb(ctx, f"at_q{i}", [P, QUAD]) for i in range(2)]
        k_r = [sh.sb(ctx, f"at_k{i}", [P, QUAD]) for i in range(2)]
        k_bd = [sh.sb(ctx, f"at_k_bd{i}", [P, HEADS, QUAD]) for i in range(2)]
        v_bd = [sh.sb(ctx, f"at_v_bd{i}", [P, 4, 4, 2 * HD]) for i in range(3)]
        prob = [[sh.sb(ctx, f"at_prob{i}{p}", [P, HEADS, WIN]) for p in range(2)] for i in range(2)]
        prob_t = [sh.sb(ctx, f"at_prob_t{p}", [P, 4, P]) for p in range(2)]
        top = [sh.sb(ctx, f"at_top{p}", [P, HEADS]) for p in range(2)]
        total = [sh.sb(ctx, f"at_total{p}", [P, HEADS]) for p in range(2)]
        inv = [[sh.sb(ctx, f"at_inv{i}{p}", [P, HEADS]) for p in range(2)] for i in range(2)]
        o_buf = [sh.sb(ctx, f"at_o{i}", [P, 16 * SIDE]) for i in range(2)]
        ps_q, ps_k, ps_s, ps_t, ps_p = sh.bank[0], sh.bank[1], sh.bank[3:5], sh.bank[5:7], sh.bank[7]
        ps_v, ps_o = sh.bank[2][:, 0:QUAD], sh.bank[2][:, QUAD:2 * QUAD]

        s = {n: sh.sem(f"at_{n}") for n in (
            "w_in", "w_hi", "w_lo", "bv_done", "b_out", "zeroed", "xn", "xn_hi", "xn_lo", "v", "k",
            "qk", "k_turned", "q_kept", "q_turned",
            "q_r", "k_r", "v_bd", "scores", "limited", "top", "shifted", "exped", "summed", "inv",
            "normed", "turned", "copied", "pv", "o_buf", "projected", "added",
            "counted")}
        kbd_in = [sh.sem(f"at_kbd_in{i}") for i in range(2)]
        last_step = B * STEPS + 2

        def all_steps(eng, prologue, step, tail):
            def steps(row):
                for j in range(ROW_STEPS):
                    step(row.number * ROW_STEPS + j, j, row)

            def rest_of_image(b):
                with eng.Fori(0, 2) as h:
                    steps(BlockRow(b, h * 2 + 1, 1))
                    steps(BlockRow(b, h * 2 + 2, 0))
                steps(BlockRow(b, ROW_STEPS - 1, 1))

            prologue()
            steps(BlockRow(0, 0, 0))
            if B > 1:
                with eng.Fori(0, B - 1) as b:
                    rest_of_image(b)
                    steps(BlockRow(b + 1, 0, 0))
            rest_of_image(B - 1)
            tail(BlockRow(B, 0, 0))

        block = ctx.enter_context(nc.Block())

        @block.sync
        def _(sp):
            sp.dma_start(w[:, :], w_dram).then_inc(s["w_in"], 16)
            sp.dma_start(bias[:, :], b_dram).then_inc(s["w_in"], 16)
            sp.dma_start(tables[:, :], tables_dram).then_inc(s["w_in"], 16)
            sp.wait_ge(s["zeroed"], 5)

            def spread(q, i):
                sp.wait_ge(s["k_r"], q + 1)
                if not is_prologue(q):
                    sp.wait_ge(s["scores"], 2 * q - 2)
                for h in range(HEADS):
                    sp.dma_start(k_bd[i][HD * h:HD * (h + 1), h, :],
                                 k_r[i][HD * h:HD * (h + 1), :]).then_inc(kbd_in[i], 16)

            def prologue():
                spread(0, 0)
                spread(1, 1)

            all_steps(sp, prologue, lambda n, j, row: spread(n + 2, j % 2), lambda row: None)
            sp.wait_ge(kbd_in[0], 128 * (last_step // 2))
            sp.wait_ge(kbd_in[1], 128 * (last_step // 2))

        @block.gpsimd
        def _(pool):
            for i in range(3):
                pool.memset(v_bd[i][:, :, :, :], 0.0).then_inc(s["zeroed"], 1)
            for i in range(2):
                pool.memset(k_bd[i][:, :, :], 0.0).then_inc(s["zeroed"], 1)

            def split_x(q, i):
                pool.wait_ge(s["xn"], q + 1)
                pool.wait_ge(s["xn_hi"], q + 1)
                nc.gpsimd.tensor_tensor(xn_lo[i][:, :], xn[i][:, :], as_f32(xn_hi[i][:, :]),
                                        ALU.subtract).then_inc(s["xn_lo"], 1)

            def rotate_k(q, i):
                pool.wait_ge(s["k_turned"], q + 1)
                if not is_prologue(q):
                    pool.wait_ge(kbd_in[i], (q - i) * 64)
                nc.gpsimd.tensor_tensor(k_r[i][:, :], turn[2][:, :], turn[3][:, :],
                                        ALU.add).then_inc(s["k_r"], 1)

            def rotate_q(q, i):
                pool.wait_ge(s["q_kept"], q + 1)
                for m, at in ((0, T_CQ), (1, T_SQ)):
                    grid = turn[m][:, :].rearrange("p (w n) -> p w n", w=4)
                    last = nc.gpsimd.tensor_tensor(
                        grid, grid, tables[:, at:at + WIN].unsqueeze(1).broadcast_to([P, 4, WIN]), ALU.mult)
                last.then_inc(s["q_turned"], 1)
                pool.wait_ge(s["q_turned"], q + 1)
                if not is_prologue(q):
                    pool.wait_ge(s["scores"], 2 * q - 2)
                nc.gpsimd.tensor_tensor(q_r[i][:, :], turn[0][:, :], turn[1][:, :],
                                        ALU.add).then_inc(s["q_r"], 1)

            def prologue():
                for q in range(2):
                    split_x(q, q)
                    rotate_k(q, q)
                    rotate_q(q, q)
                split_x(2, 0)

            def step(n, j, row):
                i = j % 2
                rotate_k(n + 2, i)
                for p in range(2):
                    pool.wait_ge(s["inv"], 2 * n + p + 1)
                    nc.gpsimd.tensor_tensor(
                        prob[i][p][:, :, :], prob[i][p][:, :, :],
                        inv[i][p][:, :].unsqueeze(2).broadcast_to([P, HEADS, WIN]),
                        ALU.mult).then_inc(s["normed"], 1)
                split_x(n + 3, 1 - i)
                rotate_q(n + 2, i)

            all_steps(pool, prologue, step, lambda row: None)

        @block.scalar
        def _(act):
            act.wait_ge(s["w_in"], 48)
            nc.scalar.activation(w_hi[:, :], w[:, 0:4 * P], ACT.Copy).then_inc(s["w_hi"], 1)
            act.wait_ge(s["zeroed"], 3)
            act.sem_inc(s["copied"], 2)
            act.sem_inc(s["o_buf"], 1)

            def normalise_x(q, i, image, col):
                wait(act, s["qk"], q - 1)
                wait(act, s["v"], q - 1)
                for out, signal in ((xn_hi, "xn_hi"), (xn, "xn")):
                    nc.scalar.activation(out[i][:, :], sh.x[:, bass.ds(col, QUAD)], ACT.Identity,
                                         scale=sh.gscale[:, bass.ds(image, 1)],
                                         bias=sh.gshift[:, bass.ds(image, 1)]).then_inc(s[signal], 1)

            def keep_v(q, k):
                act.wait_ge(s["v"], q + 1)
                if not is_prologue(q):
                    act.wait_ge(s["pv"], q - 1)
                for half in range(2):
                    rows = slice(WIN * half, WIN * (half + 1))
                    out = v_bd[k][rows, :, :, HD * half:HD * (half + 1)]
                    last = nc.scalar.activation(
                        out, ps_v[rows, :].rearrange("p (w h d) -> p w h d", w=4, d=HD), ACT.Copy)
                last.then_inc(s["v_bd"], 1)

            def keep_q(q):
                act.wait_ge(s["qk"], q + 1)
                wait(act, s["q_r"], q)
                for m in range(2):
                    last = nc.scalar.activation(turn[m][:, :], ps_q[:, m * QUAD:(m + 1) * QUAD],
                                                ACT.Identity, bias=bias[:, m:m + 1])
                last.then_inc(s["q_kept"], 1)

            def keep_o(n, half, j):
                act.wait_ge(s["pv"], n + 2)
                o = o_buf[half][:, :].rearrange("p (r e c f) -> p r e c f", e=2, c=SIDE // 2, f=2)
                col = (16 * j + ROLL) // 2
                inside = min(8, SIDE // 2 - col)
                for e in range(2):
                    src = ps_o[:, 2 * WIN * e:2 * WIN * (e + 1)].rearrange("p (f i j) -> p i j f", f=2, j=8)
                    last = nc.scalar.activation(o[:, :, e, col:col + inside, :], src[:, :, 0:inside, :],
                                                ACT.Copy)
                    if inside < 8:
                        last = nc.scalar.activation(o[:, :, e, 0:8 - inside, :], src[:, :, inside:8, :],
                                                    ACT.Copy)
                last.then_inc(s["o_buf"], 1)

            def prologue():
                for q in range(2):
                    normalise_x(q, q, 0, q * QUAD)
                    keep_q(q)
                keep_v(0, 0)
                normalise_x(2, 0, 0, 2 * QUAD)

            def step(n, j, row):
                for p in range(2):
                    act.wait_ge(s["shifted"], n * 2 + p + 3)
                    nc.scalar.activation(prob[j % 2][p][:, :, :], prob[j % 2][p][:, :, :],
                                         ACT.Exp).then_inc(s["exped"], 1)
                    if p == 0:
                        keep_v(n + 1, (j + 1) % 3)
                        if not row.starts(j):
                            turn_back(n - 1, 0)
                            turn_back(n - 1, 1)
                keep_q(n + 2)
                if j == 1 and not row.first:
                    act.wait_ge(s["projected"], row.number * 4 - 3)
                if not row.starts(j):
                    keep_o(n - 1, row.half if j else 1 - row.half, (j - 1) % ROW_STEPS)
                normalise_x(n + 3, (j + 1) % 2, *row.ahead(j))

            def turn_back(n, p):
                act.wait_ge(s["turned"], n * 2 + p + 5)
                act.wait_ge(s["pv"], n + 1)
                nc.scalar.activation(prob_t[p][:, :, :], ps_t[p][:, :].rearrange("p (h n) -> p h n", h=4),
                                     ACT.Copy).then_inc(s["copied"], 1)

            def tail(row):
                n = B * STEPS - 1
                for p in range(2):
                    turn_back(n, p)
                keep_o(n, 1, ROW_STEPS - 1)

            all_steps(act, prologue, step, tail)

        @block.vector
        def _(dve):
            dve.wait_ge(s["w_hi"], 1)
            nc.vector.tensor_tensor(w_lo[:, :], w[:, 0:4 * P], as_f32(w_hi[:, :]),
                                    ALU.subtract).then_inc(s["w_lo"], 1)
            dve.wait_ge(s["bv_done"], 1)
            nc.vector.tensor_tensor(b_out[:, :], ps_p[:, 0:1], bias[:, 5:6], ALU.add).then_inc(s["b_out"], 1)
            dve.sem_inc(s["added"], 1)
            dve.sem_inc(s["shifted"], 2)

            def turn_k(q):
                dve.wait_ge(s["k"], q + 1)
                wait(dve, s["k_r"], q)
                for m, at in ((2, T_CK), (3, T_SK)):
                    table = tables[:, at:at + WIN].unsqueeze(1).broadcast_to([P, 4, WIN])
                    last = nc.vector.scalar_tensor_tensor(
                        turn[m][:, :].rearrange("p (w n) -> p w n", w=4),
                        ps_k[:, (m - 2) * QUAD:(m - 1) * QUAD].rearrange("p (w n) -> p w n", w=4),
                        bias[:, m:m + 1], table, ALU.add, ALU.mult)
                last.then_inc(s["k_turned"], 1)

            def step(n, j, row):
                i = j % 2
                for p in range(2):
                    dve.wait_ge(s["scores"], 2 * n + p + 1)
                    src = ps_s[p][:, :].rearrange("p (h m) -> p h m", h=HEADS)
                    dve.wait_ge(s["turned"], n * 2 + p + 1)
                    if row.masked:
                        table = tables[:, T_LIM:T_LIM + WIN].unsqueeze(1).broadcast_to([P, HEADS, WIN])
                        nc.vector.tensor_tensor(prob[i][p][:, :, :], src, table, ALU.min).then_inc(s["limited"], 1)
                        src = prob[i][p][:, :, :]
                        dve.wait_ge(s["limited"], row.b * (2 * ROW_STEPS) + 2 * j + p + 1)
                    nc.vector.reduce_max(top[p][:, :], src, AX.X).then_inc(s["top"], 1)
                    dve.wait_ge(s["top"], 2 * n + p + 1)
                    nc.vector.tensor_tensor(
                        prob[i][p][:, :, :], src,
                        top[p][:, :].unsqueeze(2).broadcast_to([P, HEADS, WIN]),
                        ALU.subtract).then_inc(s["shifted"], 1)
                turn_k(n + 2)
                if j >= 2 and not row.first:
                    add_projection(row, j - 2)
                for p in range(2):
                    dve.wait_ge(s["exped"], 2 * n + p + 1)
                    nc.vector.reduce_sum(total[p][:, :], prob[i][p][:, :, :], AX.X).then_inc(s["summed"], 1)
                    dve.wait_ge(s["summed"], 2 * n + p + 1)
                    nc.vector.reciprocal(inv[i][p][:, :], total[p][:, :]).then_inc(s["inv"], 1)

            def add_projection(row, i):
                t = row.tile_before(i)
                p = row.number * 4 - 4 + i
                dve.wait_ge(s["projected"], p + 2)
                xt = sh.x[:, bass.ds(t * TILE, TILE)]
                nc.vector.scalar_tensor_tensor(xt, ps_p[:, 0:TILE], b_out[:, 0:1], xt,
                                               ALU.add, ALU.add).then_inc(s["added"], 1)
                dve.wait_ge(s["added"], p + 2)
                nc.vector.bn_stats(sh.stats[:, bass.ds(t * 6, 6)], xt).then_inc(s["counted"], 1)

            def tail(row):
                for i in range(4):
                    add_projection(row, i)

            def prologue():
                turn_k(0)
                turn_k(1)

            all_steps(dve, prologue, step, tail)

        @block.tensor
        def _(pe):
            pe.wait_ge(s["w_in"], 48)
            nc.tensor.matmul(ps_p[:, 0:1], w_p, bias[:, 4:5], start=True, stop=True).then_inc(s["bv_done"], 1)
            pe.sem_inc(s["turned"], 4)
            pe.sem_inc(s["pv"], 1)
            pe.sem_inc(s["projected"], 1)
            pe.wait_ge(s["w_lo"], 1)
            pe.wait_ge(s["b_out"], 1)

            def project_in(q, i):
                pe.wait_ge(s["xn_hi"], q + 1)
                pe.wait_ge(s["xn_lo"], q + 1)
                wait(pe, s["k_turned"], q)
                wait(pe, s["q_kept"], q)
                for m in (2, 3, 0, 1):
                    out = (ps_q, ps_k)[m // 2][:, m % 2 * QUAD:(m % 2 + 1) * QUAD]
                    cols = slice(m * P, (m + 1) * P)
                    last = split_product(nc, out, w_hi[:, cols], w_lo[:, cols], xn_hi[i][:, :],
                                         xn_lo[i][:, :])
                    if m % 2:
                        last.then_inc(s["k" if m == 3 else "qk"], 1)

            def project_v(q, i):
                pe.wait_ge(s["xn"], q + 1)
                wait(pe, s["v_bd"], q)
                if not is_prologue(q):
                    pe.wait_ge(s["o_buf"], q - 1)
                for wdw in range(4):
                    for half in range(2):
                        last = nc.tensor.matmul(
                            ps_v[WIN * half:WIN * (half + 1), WIN * wdw:WIN * (wdw + 1)],
                            xn[i][:, WIN * wdw:WIN * (wdw + 1)], w_v[:, WIN * half:WIN * (half + 1)],
                            start=True, stop=True)
                last.then_inc(s["v"], 1)

            def score(n, i):
                pe.wait_ge(s["q_r"], n + 1)
                pe.wait_ge(kbd_in[i], (n - i) * 64 + 128)
                for wdw in range(4):
                    p = wdw // 2
                    if wdw % 2 == 0:
                        pe.wait_ge(s["shifted"], n * 2 + p + 1)
                    rows = slice(WIN * (wdw % 2), WIN * (wdw % 2 + 1))
                    last = nc.tensor.matmul(
                        ps_s[p][rows, :].rearrange("p (h m) -> p h m", h=HEADS),
                        q_r[i][:, WIN * wdw:WIN * (wdw + 1)],
                        k_bd[i][:, :, WIN * wdw:WIN * (wdw + 1)], start=True, stop=True)
                    if wdw % 2:
                        last.then_inc(s["scores"], 1)

            def turn_probs(n, i):
                for p in range(2):
                    pe.wait_ge(s["normed"], n * 2 + p + 1)
                    pe.wait_ge(s["copied"], n * 2 + p + 1)
                    for hp in range(4):
                        last = nc.tensor.transpose(
                            ps_t[p][:, hp * P:(hp + 1) * P],
                            prob[i][p][:, 2 * hp:2 * hp + 2, :].rearrange("p h m -> p (h m)"),
                            sh.const[:, C_ID:C_ID + P])
                    last.then_inc(s["turned"], 1)

            def weigh(n, k):
                pe.wait_ge(s["copied"], n * 2 + 4)
                ahead = min(n + 3, B * STEPS + 1) if isinstance(n, int) else n + 3
                pe.wait_ge(s["v_bd"], ahead)
                pe.wait_ge(s["o_buf"], n + 1)
                for wdw in range(4):
                    for hp in range(4):
                        last = nc.tensor.matmul(
                            ps_o[32 * hp:32 * (hp + 1), WIN * wdw:WIN * (wdw + 1)], v_bd[k][:, wdw, hp, :],
                            prob_t[wdw // 2][:, hp, WIN * (wdw % 2):WIN * (wdw % 2 + 1)],
                            start=True, stop=True)
                last.then_inc(s["pv"], 1)

            def prologue():
                project_in(0, 0)
                project_in(1, 1)
                project_v(0, 0)

            def project(row, i):
                pe.wait_ge(s["o_buf"], row.number * ROW_STEPS + 1)
                pe.wait_ge(s["added"], row.number * 4 - 3 + i)
                nc.tensor.matmul(ps_p[:, 0:TILE], w_p, o_buf[1 - row.half][:, i * TILE:(i + 1) * TILE],
                                 start=True, stop=True).then_inc(s["projected"], 1)

            def step(n, j, row):
                score(n, j % 2)
                project_v(n + 1, (j + 1) % 2)
                if not row.starts(j):
                    turn_probs(n - 1, (j + 1) % 2)
                project_in(n + 2, j % 2)
                if not row.starts(j):
                    weigh(n - 1, (j + 2) % 3)
                if 1 <= j <= 4 and not row.first:
                    project(row, j - 1)

            def tail(row):
                n = B * STEPS - 1
                turn_probs(n, 1)
                weigh(n, 2)
                for i in range(4):
                    project(row, i)

            all_steps(pe, prologue, step, tail)


TAPS = [(dy, dx) for dy in (-1, 0, 1) for dx in (-1, 0, 1)]


def walk_groups(eng, groups, body):
    with eng.Fori(0, groups - 1) as g:
        body(g)
    body(groups - 1)


def group_tables(nc, sh, link, per_image, scale, shift):
    for out, src in ((scale, sh.gscale), (shift, sh.gshift)):
        link(nc.vector.tensor_copy(
            out[:, :].rearrange("p (b g) -> p b g", g=per_image),
            src[:, 0:sh.images].unsqueeze(2).broadcast_to([P, sh.images, per_image])))


def conv1_stage(sh, w_dram, b_dram, y_dram):
    nc = sh.nc
    groups = sh.images * TILES // R1
    tiles = groups * R1
    first_flag, last_flag = (sh.const[:, C_F1 + i * groups:C_F1 + (i + 1) * groups] for i in range(2))
    rows = R1 * TR + 2
    with ExitStack() as ctx:
        w = sh.sb(ctx, "c1_w", [P, 9, P])
        w_hi = sh.sb(ctx, "c1_w_hi", [P, 9, P], F32R)
        w_lo = sh.sb(ctx, "c1_w_lo", [P, 9, P], F32R)
        bias = sh.sb(ctx, "c1_bias", [P, 1])
        scale, shift = (sh.sb(ctx, f"c1_{n}", [P, groups]) for n in ("scale", "shift"))
        xn = [sh.sb(ctx, f"c1_xn{i}", [P, TILE]) for i in range(2)]
        ring_hi = sh.sb(ctx, "c1_ring_hi", [P, rows, PITCH], F32R)
        ring_lo = sh.sb(ctx, "c1_ring_lo", [P, rows, PITCH], F32R)
        y = sh.sb(ctx, "c1_y", [P, R1, TILE])
        s = {n: sh.sem(f"c1_{n}") for n in (
            "w_in", "w_masked", "w_hi", "w_lo", "chain", "xn", "hi", "lo", "mirrored", "conv",
            "y_kept", "counted")}
        y_out = [sh.sem(f"c1_y_out{i}") for i in range(R1)]

        def slot_rows(j):
            return slice(1 + TR * j, 1 + TR * (j + 1))

        block = ctx.enter_context(nc.Block())

        @block.sync
        def _(sp):
            sp.dma_start(w[:, :, :], w_dram).then_inc(s["w_in"], 16)
            sp.dma_start(bias[:, :], b_dram).then_inc(s["w_in"], 16)
            for i in range(R1):
                sp.sem_inc(y_out[i], 16)
            with sp.Fori(0, groups) as g:
                for j in range(R1):
                    t = g * R1 + j
                    sp.wait_ge(s["y_kept"], t + 1 + R1)
                    sp.dma_start(y_dram[:, bass.ds(t * TILE, TILE)], y[:, j, :]).then_inc(y_out[j], 16)
            for i in range(R1):
                sp.wait_ge(y_out[i], 16 * (groups + 1))

        @block.gpsimd
        def _(pool):
            nc.gpsimd.memset(as_f32(ring_hi[:, :, :]), 0.0)
            nc.gpsimd.memset(as_f32(ring_lo[:, :, :]), 0.0).then_inc(s["mirrored"], 1)

            def mirror(t, g, j):
                if j not in (0, R1 - 1):
                    return
                src, dst, flag = (1, rows - 1, first_flag) if j == 0 else (R1 * TR, 0, last_flag)
                pool.wait_ge(s["hi"], t + 1)
                pool.wait_ge(s["lo"], t + 1)
                for ring in (ring_hi, ring_lo):
                    last = nc.gpsimd.tensor_tensor(ring[:, dst, :], as_f32(ring[:, src, :]),
                                                   flag[:, bass.ds(g, 1)].broadcast_to([P, PITCH]), ALU.mult)
                last.then_inc(s["mirrored"], 1)

            for t in range(2):
                mirror(t, 0, t)

            def body(g):
                for j in range(R1):
                    t = g * R1 + j + 2
                    if not (isinstance(t, int) and t >= tiles):
                        mirror(t, g + (j + 2) // R1, (j + 2) % R1)

            walk_groups(pool, groups, body)
            pool.wait_ge(s["conv"], tiles - R1 + 3)
            nc.gpsimd.memset(as_f32(ring_hi[:, rows - 1, :]), 0.0)
            nc.gpsimd.memset(as_f32(ring_lo[:, rows - 1, :]), 0.0).then_inc(s["mirrored"], 1)

        @block.scalar
        def _(act):
            act.wait_ge(s["w_masked"], 1)
            nc.scalar.activation(w_hi[:, :, :], w[:, :, :], ACT.Copy).then_inc(s["w_hi"], 1)
            act.sem_inc(s["y_kept"], R1)
            act.wait_ge(s["mirrored"], 1)
            act.wait_ge(s["chain"], 2)

            def hi(t, g, j):
                wait(act, s["conv"], t + 1)
                wait(act, s["lo"], t - 1)
                if j == 0:
                    wait(act, s["mirrored"], g * 2)
                nc.scalar.activation(
                    ring_hi[:, slot_rows(j), 1:1 + SIDE],
                    sh.x[:, bass.ds(t * TILE, TILE)].rearrange("p (r c) -> p r c", c=SIDE),
                    ACT.Identity, scale=scale[:, bass.ds(g, 1)],
                    bias=shift[:, bass.ds(g, 1)]).then_inc(s["hi"], 1)
                nc.scalar.activation(xn[j % 2][:, :], sh.x[:, bass.ds(t * TILE, TILE)], ACT.Identity,
                                     scale=scale[:, bass.ds(g, 1)],
                                     bias=shift[:, bass.ds(g, 1)]).then_inc(s["xn"], 1)

            for t in range(2):
                hi(t, 0, t)

            def body(g):
                for j in range(R1):
                    t = g * R1 + j
                    if not (isinstance(t, int) and t + 2 >= tiles):
                        hi(t + 2, g + (j + 2) // R1, (j + 2) % R1)
                    act.wait_ge(s["conv"], t + 1 + 3)
                    act.wait_ge(y_out[j], g * 16 + 16)
                    act.wait_ge(s["counted"], t + 1)
                    nc.scalar.activation(y[:, j, :], sh.bank[j][:, 0:TILE], ACT.Identity,
                                         bias=bias[:, 0:1]).then_inc(s["y_kept"], 1)

            walk_groups(act, groups, body)

        @block.vector
        def _(dve):
            link = Chain(dve, s["chain"])
            group_tables(nc, sh, link, TILES // R1, scale, shift)
            dve.wait_ge(s["w_in"], 32)
            nc.vector.scalar_tensor_tensor(
                w[:, :, :], w[:, :, :], 4.0,
                sh.const[:, C_GAVG:C_GAVG + P].unsqueeze(1).broadcast_to([P, 9, P]),
                ALU.mult, ALU.mult).then_inc(s["w_masked"], 1)
            dve.wait_ge(s["w_hi"], 1)
            nc.vector.tensor_tensor(w_lo[:, :, :], w[:, :, :], as_f32(w_hi[:, :, :]),
                                    ALU.subtract).then_inc(s["w_lo"], 1)
            dve.sem_inc(s["counted"], R1)

            def lo(t, i, j):
                dve.wait_ge(s["xn"], t + 1)
                dve.wait_ge(s["hi"], t + 1)
                at = (slice(None), slot_rows(j), slice(1, 1 + SIDE))
                nc.vector.tensor_tensor(
                    ring_lo[at], xn[i][:, :].rearrange("p (r c) -> p r c", c=SIDE),
                    as_f32(ring_hi[:, :, :])[at], ALU.subtract).then_inc(s["lo"], 1)

            for t in range(2):
                lo(t, t, t)

            def body(g):
                for j in range(R1):
                    t = g * R1 + j
                    if not (isinstance(t, int) and t + 2 >= tiles):
                        lo(t + 2, j % 2, (j + 2) % R1)
                    dve.wait_ge(s["y_kept"], t + 1 + R1)
                    nc.vector.bn_stats(sh.stats[:, bass.ds(t * 6, 6)], y[:, j, :]).then_inc(s["counted"], 1)

            walk_groups(dve, groups, body)

        @block.tensor
        def _(pe):
            pe.sem_inc(s["conv"], 3)
            pe.wait_ge(s["w_lo"], 1)

            def body(g):
                for j in range(R1):
                    t = g * R1 + j
                    ready = min(t + 2, tiles) if isinstance(t, int) else t + 2
                    pe.wait_ge(s["hi"], ready)
                    pe.wait_ge(s["lo"], ready)
                    if j == 0:
                        pe.wait_ge(s["mirrored"], g * 2 + 1)
                    if j == R1 - 1:
                        pe.wait_ge(s["mirrored"], g * 2 + 4)
                    pe.wait_ge(s["y_kept"], t + 1)
                    out = sh.bank[j][:, 0:TILE].rearrange("p (r c) -> p r c", c=SIDE)
                    for n, (dy, dx) in enumerate(TAPS):
                        at = (slice(None), slice(1 + TR * j + dy, 1 + TR * (j + 1) + dy),
                              slice(1 + dx, 1 + dx + SIDE))
                        last = split_product(nc, out, w_hi[:, n, :], w_lo[:, n, :], ring_hi[at],
                                             ring_lo[at], start=n == 0, stop=n == 8)
                    last.then_inc(s["conv"], 1)

            walk_groups(pe, groups, body)


APPLY_T = 3
APPLY_RING = 4


def batch_norm_stage(sh, gb_dram, y_dram):
    nc = sh.nc
    tiles = sh.images * TILES
    width = APPLY_T * TILE
    rounds = tiles // (APPLY_T * APPLY_RING)
    with ExitStack() as ctx:
        gb = sh.sb(ctx, "bn_gb", [P, 2])
        agg = sh.sb(ctx, "bn_agg", [P, 2])
        t1, t2, scale, shift = (sh.sb(ctx, f"bn_{n}", [P, 1]) for n in ("t1", "t2", "scale", "shift"))
        y = sh.sb(ctx, "bn_y", [P, APPLY_RING, width])
        s = {n: sh.sem(f"bn_{n}") for n in (
            "gb_in", "chain", "asked", "rooted", "ready", "relu", "counted")}
        added = [sh.sem(f"bn_added{i}") for i in range(APPLY_RING)]
        on_pool = (1, 3)
        y_in = [sh.sem(f"bn_y_in{i}") for i in range(APPLY_RING)]
        block = ctx.enter_context(nc.Block())

        @block.sync
        def _(sp):
            sp.dma_start(gb[:, :], gb_dram).then_inc(s["gb_in"], 16)
            with sp.Fori(0, rounds) as g:
                for j in range(APPLY_RING):
                    n = g * APPLY_RING + j
                    sp.wait_ge(added[j], g + 1)
                    sp.dma_start(y[:, j, :], y_dram[:, bass.ds(n * width, width)]).then_inc(y_in[j], 16)

        @block.gpsimd
        def _(pool):
            with pool.Fori(0, rounds) as g:
                for j in on_pool:
                    n = g * APPLY_RING + j
                    pool.wait_ge(s["relu"], n + 1)
                    xt = sh.x[:, bass.ds(n * width, width)]
                    nc.gpsimd.tensor_tensor(xt, xt, y[:, j, :], ALU.add).then_inc(added[j], 1)

        @block.scalar
        def _(act):
            act.wait_ge(s["asked"], 1)
            nc.scalar.activation(t2[:, :], t1[:, :], ACT.Sqrt).then_inc(s["rooted"], 1)
            act.wait_ge(s["ready"], 1)
            with act.Fori(0, rounds) as g:
                for j in range(APPLY_RING):
                    act.wait_ge(y_in[j], g * 16 + 16)
                    nc.scalar.activation(y[:, j, :], y[:, j, :], ACT.Relu, scale=scale[:, 0:1],
                                         bias=shift[:, 0:1]).then_inc(s["relu"], 1)

        @block.vector
        def _(dve):
            link = Chain(dve, s["chain"])
            for j in range(APPLY_RING):
                dve.sem_inc(added[j], 1)
            link(nc.vector.bn_aggr(agg[:, :], sh.stats[:, 0:tiles * 6]))

            def act_sqrt(out, v):
                dve.sem_inc(s["asked"], 1)
                dve.wait_ge(s["rooted"], 1)

            rsqrt_steps(nc, link, act_sqrt, scale[:, :], agg[:, 1:2], t1[:, :], t2[:, :], 1e-5)
            dve.wait_ge(s["gb_in"], 16)
            link(nc.vector.tensor_tensor(scale[:, :], scale[:, :], gb[:, 0:1], ALU.mult))
            link(nc.vector.tensor_tensor(t1[:, :], agg[:, 0:1], scale[:, :], ALU.mult))
            nc.vector.tensor_tensor(shift[:, :], gb[:, 1:2], t1[:, :], ALU.subtract).then_inc(s["ready"], 1)
            with dve.Fori(0, rounds) as g:
                for j in range(APPLY_RING):
                    n = g * APPLY_RING + j
                    if j not in on_pool:
                        dve.wait_ge(s["relu"], n + 1)
                        xt = sh.x[:, bass.ds(n * width, width)]
                        nc.vector.tensor_tensor(xt, xt, y[:, j, :], ALU.add).then_inc(added[j], 1)
                    dve.wait_ge(added[j], g + 2)
                    for i in range(APPLY_T):
                        nc.vector.bn_stats(
                            sh.stats[:, bass.ds(n * (6 * APPLY_T) + 6 * i, 6)],
                            sh.x[:, bass.ds(n * width + i * TILE, TILE)]).then_inc(s["counted"], 1)


W_1, W_1B, W_B1, W_2, W_2S, W_B2, W_3R, W_3C, W_B3, W_END = (
    0, 32, 160, 161, 449, 737, 738, 866, 867, 868)

COPIES = ((-1, 1, None, 0), (-1, 1, 0), (-1, 0, 1))


def block_rows(i):
    return slice(32 * i, 32 * (i + 1))


def out_rows(i):
    return block_rows(3 - i)


def stack_stage(sh, tag, w_dram, out_dram=None):
    nc = sh.nc
    groups = sh.images * TILES // BODY
    tiles = groups * BODY
    at = C_F1 + 2 * (sh.images * TILES // R1)
    first_flag, last_flag = (sh.const[:, at + i * groups:at + (i + 1) * groups] for i in range(2))
    a_rows = R2 * TR + 2
    z_rows = R2 * TR
    with ExitStack() as ctx:
        def sb(name, shape, dt=F32):
            return sh.sb(ctx, f"{tag}_{name}", shape, dt)

        m1_hi, m1_lo = sb("m1_hi", [P, P], F32R), sb("m1_lo", [P, P], F32R)
        m3_hi, m3_lo = sb("m3_hi", [P, P], F32R), sb("m3_lo", [P, P], F32R)
        u_hi, u_lo = sb("u_hi", [P, 9, P], F32R), sb("u_lo", [P, 9, P], F32R)
        v_hi, v_lo = ([sb(f"v_{n}{j}", [32 * len(COPIES[j]), 3, 32 * (3 - j)], F32R) for j in range(3)]
                      for n in ("hi", "lo"))
        c1, c3, b2 = sb("c1", [P, 1]), sb("c3", [P, 1]), sb("b2", [P, 1])
        scale, shift, scale1, shift3 = (sb(n, [P, groups]) for n in ("scale", "shift", "scale1", "shift3"))
        s = {n: sh.sem(f"{tag}_{n}") for n in (
            "w_in", "chain", "pe_chain", "zeroed", "placed", "z_zeroed", "xn", "xn_hi", "xn_lo", "s1",
            "a_hi", "a_lo", "mirrored",
            "s2", "s4", "s6", "s8", "sum0", "sum1", "sum2", "sum3", "z0_hi", "z1_hi", "z2_hi", "z0_lo",
            "z1_lo", "z2_lo", "z0_edge", "z1_edge", "z2_edge", "r_hi", "r_lo", "f", "x_scaled",
            "updated", "counted")}
        if out_dram is not None:
            s.update({n: sh.sem(f"{tag}_{n}") for n in ("out_turned", "out_kept", "stored")})
            result, ps_out = sh.stats[:, 0:TILE], sh.bank[5][:, 0:TILE]
            out_v = out_dram.rearrange("(t q p) c -> t p q c", q=TILE // P, p=P)

        z_copied = [[sh.sem(f"{tag}_z{i}_copied{p}") for p in range(2)] for i in range(3)]

        with ExitStack() as prep:
            w = sh.sb(prep, f"{tag}_w", [P, W_END])
            d = sh.sb(prep, f"{tag}_d", [32, 4, P + 1])
            d0 = sh.sb(prep, f"{tag}_d0", [P, P])
            d1 = sh.sb(prep, f"{tag}_d1", [P, P])
            d2 = sh.sb(prep, f"{tag}_d2", [P, P])

            def placements():
                places = [(u_hi, u_lo, block_rows(q), slice(32 * (3 - q), P), W_2, 9) for q in range(4)]
                places += [(v_hi[j], v_lo[j], slice(0, 32 * len(COPIES[j])), slice(0, 32 * (3 - j)),
                            W_2S + 96 * j, 3) for j in range(3)]
                for hi, lo, rows, cols, at, taps in places:
                    hi, lo = (x[rows, :, cols].rearrange("p t (b e) -> p t b e", e=32) for x in (hi, lo))
                    src = w[rows, at:at + 32 * taps].rearrange("p (t e) -> p t e", e=32)
                    yield hi, lo, src.unsqueeze(2).broadcast_to(list(hi.shape))

            block = prep.enter_context(nc.Block())

            @block.sync
            def _(sp):
                sp.dma_start(w[:, :], w_dram).then_inc(s["w_in"], 16)

            @block.gpsimd
            def _(pool):
                for m in (u_hi, u_lo, *v_hi, *v_lo):
                    last = nc.gpsimd.memset(as_f32(m[tuple([slice(None)] * len(m.shape))]), 0.0)
                last.then_inc(s["zeroed"], 1)

            @block.tensor
            def _(pe):
                pe.wait_ge(s["w_in"], 16)
                nc.tensor.transpose(sh.bank[0][0:32, 0:P], w[:, W_1:W_1 + 32],
                                    sh.const[:, C_ID:C_ID + P]).then_inc(s["pe_chain"], 1)
                for i in range(3):
                    pe.wait_ge(s["chain"], 4 + 2 * i)
                    nc.tensor.matmul(sh.bank[1 + i][0:32, 0:P + 1], w[0:32, W_1B + 32 * i:W_1B + 32 * (i + 1)],
                                     d[:, i, :], start=True, stop=True).then_inc(s["pe_chain"], 1)
                pe.wait_ge(s["chain"], 10)
                for i in range(4):
                    last = nc.tensor.transpose(sh.bank[4][:, 32 * i:32 * (i + 1)], d[:, i, 0:P],
                                               sh.const[0:32, C_ID:C_ID + 32])
                last.then_inc(s["pe_chain"], 1)

            @block.vector
            def _(dve):
                link = Chain(dve, s["chain"])
                group_tables(nc, sh, link, TILES // BODY, scale, shift)
                dve.wait_ge(s["w_in"], 16)
                dve.wait_ge(s["pe_chain"], 1)
                link(nc.vector.tensor_copy(d[:, 0, 0:P], sh.bank[0][0:32, 0:P]))
                link(nc.vector.tensor_copy(d[:, 0, P:P + 1], w[0:32, W_B1:W_B1 + 1]))
                for i in range(3):
                    dve.wait_ge(s["pe_chain"], 2 + i)
                    link(nc.vector.tensor_tensor(d[:, i + 1, :], d[:, i, :], sh.bank[1 + i][0:32, 0:P + 1], ALU.add))
                    own = slice(32 * i, 32 * (i + 1))
                    link(nc.vector.tensor_tensor(d[:, i + 1, own], d[:, i + 1, own], d[:, 0, own], ALU.subtract))
                for i in range(4):
                    link(nc.vector.tensor_copy(c1[32 * i:32 * (i + 1), :], d[:, i, P:P + 1]))
                dve.wait_ge(s["pe_chain"], 5)
                link(nc.vector.tensor_copy(m1_hi[:, :], sh.bank[4][:, 0:P]))
                link(nc.vector.tensor_tensor(m1_lo[:, :], sh.bank[4][:, 0:P], as_f32(m1_hi[:, :]), ALU.subtract))
                w3 = w[:, W_3R:W_3R + P - 1]
                link(nc.vector.memset(d0[:, 0:1], 1.0))
                link(nc.vector.tensor_scalar(d0[:, 1:P], w3, 1.0, None, ALU.add))
                link(nc.vector.memset(d1[:, 0:1], 0.0))
                link(nc.vector.scalar_tensor_tensor(d1[:, 1:P], w3, -1.0, sh.const[:, C_ID:C_ID + P - 1],
                                                    ALU.mult, ALU.mult))
                link(nc.vector.tensor_tensor_scan(d2[:, :], d0[:, :], d1[:, :], w[:, W_3C:W_3C + 1],
                                                  ALU.mult, ALU.add))
                for i in range(4):
                    link(nc.vector.tensor_copy(d1[out_rows(i), :], d2[block_rows(i), :]))
                link(nc.vector.tensor_copy(m3_hi[:, :], d1[:, :]))
                link(nc.vector.tensor_tensor(m3_lo[:, :], d1[:, :], as_f32(m3_hi[:, :]), ALU.subtract))
                link(nc.vector.memset(d1[:, :], 0.0))
                link(nc.vector.tensor_tensor_scan(d2[:, :], d0[:, :], d1[:, :], w[:, W_B3:W_B3 + 1],
                                                  ALU.mult, ALU.add))
                link(nc.vector.tensor_tensor(d2[:, :], d2[:, :], sh.const[:, C_ID:C_ID + P], ALU.mult))
                link(nc.vector.reduce_sum(c3[:, :], d2[:, :], AX.X))
                link(nc.vector.tensor_scalar(scale1[:, :], scale[:, :], 1.0, None, ALU.add))
                link(nc.vector.tensor_scalar(shift3[:, :], shift[:, :], c3[:, 0:1], None, ALU.add))
                link(nc.vector.tensor_copy(b2[:, :], w[:, W_B2:W_B2 + 1]))

                dve.wait_ge(s["placed"], 1)
                for hi, lo, src in placements():
                    link(nc.vector.tensor_tensor(lo, src, as_f32(hi), ALU.subtract))

            @block.scalar
            def _(act):
                act.wait_ge(s["w_in"], 16)
                act.wait_ge(s["zeroed"], 1)
                for hi, lo, src in placements():
                    last = nc.scalar.activation(hi, src, ACT.Copy)
                last.then_inc(s["placed"], 1)

        xn = sb("xn", [P, TILE])
        xn_hi = [sb(f"xn_hi{i}", [P, TILE], F32R) for i in range(2)]
        xn_lo = [sb(f"xn_lo{i}", [P, TILE], F32R) for i in range(2)]
        a_f = sb("a_f", [P, TILE])
        a_hi, a_lo = (sb(n, [P, a_rows, PITCH], F32R) for n in ("ring_a_hi", "ring_a_lo"))
        acc = sb("acc", [P, BODY, TILE])
        z = [sb(f"ring_z{i}", [32 * len(COPIES[i]), 2, z_rows, PITCH], F32R) for i in range(3)]
        r_hi, r_lo = sb("r_hi", [P, TILE], F32R), sb("r_lo", [P, TILE], F32R)
        ps_d, ps_z, ps_a, ps_f = sh.bank[0:2], sh.bank[2:5], sh.bank[6], sh.bank[7]
        inner = slice(1, 1 + SIDE)

        def grid(ap):
            return ap.rearrange("p (r c) -> p r c", c=SIDE)

        def valid(t):
            return not isinstance(t, int) or 0 <= t < tiles

        def upto(t):
            return min(t, tiles) if isinstance(t, int) else t

        def group_of(g, j, lag):
            return g + (j - lag) // BODY

        def walk(eng, step):
            def steps(first, end):
                for k in range(first, end):
                    g = (k - 1) // BODY
                    step(g, k - g * BODY, k)

            steps(-3, BODY + 1)
            with eng.Fori(1, groups - 1) as g:
                for j in range(1, BODY + 1):
                    step(g, j, g * BODY + j)
            steps(tiles - BODY + 1, tiles + 7)

        block = ctx.enter_context(nc.Block())

        @block.sync
        def _(sp):
            def copy_z(i, t, jt):
                if not valid(t):
                    return
                zi, slot = as_f32(z[i][:, :, :, :]), jt % R2
                r0 = TR * slot
                own, down, up = (block_rows(COPIES[i].index(dy)) for dy in (0, -1, 1))
                n_down = TR if slot < R2 - 1 else TR - 1
                first_up = 0 if slot else 1
                sp.wait_ge(s[f"z{i}_lo"], t + 1)
                sp.dma_start(zi[down, :, r0 + 1:r0 + 1 + n_down, :],
                             zi[own, :, r0:r0 + n_down, :]).then_inc(z_copied[i][jt % 2], 16)
                sp.dma_start(zi[up, :, r0 - 1 + first_up:r0 - 1 + TR, :],
                             zi[own, :, r0 + first_up:r0 + TR, :]).then_inc(z_copied[i][jt % 2], 16)

            def step(g, j, k):
                copy_z(2, k - 4, (j - 4) % BODY)
                copy_z(1, k - 2, (j - 2) % BODY)
                copy_z(0, k, j % BODY)
                t = k - 7
                if out_dram is not None and valid(t):
                    sp.wait_ge(s["out_kept"], t + 2)
                    sp.dma_start(out_v[bass.ds(t, 1)].rearrange("o p q c -> (o p) q c"),
                                 sh.x[:, bass.ds(t * TILE, TILE)].rearrange("p (q c) -> p q c", c=P))\
                        .then_inc(s["stored"], 16)

            walk(sp, step)
            if out_dram is not None:
                sp.wait_ge(s["stored"], 16 * tiles)

        @block.gpsimd
        def _(pool):
            nc.gpsimd.memset(as_f32(a_hi[:, :, :]), 0.0)
            nc.gpsimd.memset(as_f32(a_lo[:, :, :]), 0.0).then_inc(s["mirrored"], 1)

            def step(g, j, k):
                t, jt = k + 2, (j + 2) % BODY
                if valid(t) and jt % R2 != 1:
                    src, dst = (1, a_rows - 1) if jt % R2 == 0 else (R2 * TR, 0)
                    gt = group_of(g, j, -2)
                    flag = {0: first_flag[:, bass.ds(gt, 1)], BODY - 1: last_flag[:, bass.ds(gt, 1)]}.get(
                        jt, sh.const[:, C_ONE:C_ONE + 1])
                    pool.wait_ge(s["a_hi"], t + 1)
                    pool.wait_ge(s["a_lo"], t + 1)
                    for ring in (a_hi, a_lo):
                        last = nc.gpsimd.tensor_tensor(ring[:, dst, :], as_f32(ring[:, src, :]),
                                                       flag.broadcast_to([P, PITCH]), ALU.mult)
                    last.then_inc(s["mirrored"], 1)
                if isinstance(t, int) and t == tiles:
                    pool.wait_ge(s["s2"], tiles - R2)
                    nc.gpsimd.memset(as_f32(a_hi[:, a_rows - 1, :]), 0.0)
                    nc.gpsimd.memset(as_f32(a_lo[:, a_rows - 1, :]), 0.0).then_inc(s["mirrored"], 1)
                t, i = k + 3, (j + 3) % 2
                if valid(t):
                    pool.wait_ge(s["xn"], t + 1)
                    pool.wait_ge(s["xn_hi"], t + 1)
                    wait(pool, s["s1"], t - 1)
                    nc.gpsimd.tensor_tensor(xn_lo[i][:, :], xn[:, :], as_f32(xn_hi[i][:, :]),
                                            ALU.subtract).then_inc(s["xn_lo"], 1)

            walk(pool, step)

        @block.scalar
        def _(act):
            act.wait_ge(s["mirrored"], 1)
            act.wait_ge(s["z_zeroed"], 1)

            def high_z(i, t, jt):
                if valid(t):
                    act.wait_ge(s[f"sum{i}"], t + 1)
                    r0, own = TR * (jt % R2), out_rows(i)
                    nc.scalar.activation(z[i][own, 0, r0:r0 + TR, inner], grid(acc[own, jt, :]),
                                         ACT.Copy).then_inc(s[f"z{i}_hi"], 1)

            def step(g, j, k):
                t, jt = k - 6, j % BODY
                if valid(t):
                    act.wait_ge(s["sum3"], t + 1)
                    wait(act, s["f"], t)
                    nc.scalar.activation(r_hi[:, :], acc[:, jt, :], ACT.Relu).then_inc(s["r_hi"], 1)
                    gt = group_of(g, j, 6)
                    xt = sh.x[:, bass.ds(t * TILE, TILE)]
                    nc.scalar.activation(xt, xt, ACT.Identity, scale=scale1[:, bass.ds(gt, 1)],
                                         bias=shift3[:, bass.ds(gt, 1)]).then_inc(s["x_scaled"], 1)
                high_z(2, k - 4, (j - 4) % BODY)
                t, jt = k + 2, (j + 2) % BODY
                if valid(t):
                    act.wait_ge(s["s1"], t + 1)
                    r0 = 1 + TR * (jt % R2)
                    nc.scalar.activation(a_hi[:, r0:r0 + TR, inner], grid(ps_a[:, 0:TILE]), ACT.Relu,
                                         bias=c1[:, 0:1])
                    wait(act, s["a_lo"], t)
                    nc.scalar.activation(a_f[:, :], ps_a[:, 0:TILE], ACT.Relu,
                                         bias=c1[:, 0:1]).then_inc(s["a_hi"], 1)
                high_z(1, k - 2, (j - 2) % BODY)
                if valid(k):
                    act.wait_ge(s["s2"], k + 1)
                    if not isinstance(k, int) or k >= BODY:
                        act.wait_ge(s["r_lo"], k - BODY + 1)
                    nc.scalar.activation(acc[:, j % BODY, :], ps_d[j % 2][:, 0:TILE], ACT.Identity,
                                         bias=b2[:, 0:1]).then_inc(s["sum0"], 1)
                    high_z(0, k, j % BODY)
                t, i = k + 3, (j + 3) % 2
                if valid(t):
                    gt = group_of(g, j, -3)
                    wait(act, s["s1"], t - 1)
                    wait(act, s["xn_lo"], t)
                    for out, signal in ((xn_hi[i], "xn_hi"), (xn, "xn")):
                        nc.scalar.activation(out[:, :], sh.x[:, bass.ds(t * TILE, TILE)], ACT.Identity,
                                             scale=scale[:, bass.ds(gt, 1)],
                                             bias=shift[:, bass.ds(gt, 1)]).then_inc(s[signal], 1)

            walk(act, step)

        @block.vector
        def _(dve):
            for i in range(3):
                last = nc.vector.memset(as_f32(z[i][:, :, :, :]), 0.0)
            last.then_inc(s["z_zeroed"], 1)
            dve.wait_ge(s["z_zeroed"], 1)
            dve.wait_ge(s["mirrored"], 1)
            if out_dram is not None:
                dve.sem_inc(s["out_kept"], 1)
                dve.sem_inc(s["out_turned"], 1)

            def add_up(i, t, jt):
                if valid(t):
                    dve.wait_ge(s[("s4", "s6", "s8")[i - 1]], t + 1)
                    dve.wait_ge(s[f"sum{i - 1}"], t + 1)
                    rows = slice(0, 32 * (4 - i))
                    nc.vector.tensor_tensor(acc[rows, jt, :], acc[rows, jt, :], ps_z[i - 1][rows, 0:TILE],
                                            ALU.add).then_inc(s[f"sum{i}"], 1)

            def low_z(i, g, j, lag):
                t, jt = g * BODY + (j - lag), (j - lag) % BODY
                gt = group_of(g, j, lag)
                if not valid(t):
                    return
                zi, slot = z[i], jt % R2
                r0 = TR * slot
                own, down, up = (block_rows(COPIES[i].index(dy)) for dy in (0, -1, 1))
                dve.wait_ge(s[f"z{i}_hi"], t + 1)
                nc.vector.tensor_tensor(zi[own, 1, r0:r0 + TR, inner], grid(acc[own, jt, :]),
                                        as_f32(zi[own, 0, r0:r0 + TR, inner]), ALU.subtract)\
                    .then_inc(s[f"z{i}_lo"], 1)
                mid = as_f32(zi[own, :, :, :])
                if slot == R2 - 1:
                    dve.wait_ge(s[f"z{i}_lo"], t + 1)
                    flag = last_flag[own, bass.ds(gt, 1)] if jt == BODY - 1 else 1.0
                    nc.vector.tensor_scalar(zi[down, :, 0, inner], mid[:, :, z_rows - 1, inner], flag,
                                            None, ALU.mult).then_inc(s[f"z{i}_edge"], 1)
                if slot == 0:
                    dve.wait_ge(s[f"z{i}_lo"], t + 1)
                    flag = first_flag[own, bass.ds(gt, 1)] if jt == 0 else 1.0
                    nc.vector.tensor_scalar(zi[up, :, z_rows - 1, inner], mid[:, :, 0, inner], flag,
                                            None, ALU.mult).then_inc(s[f"z{i}_edge"], 1)
                if isinstance(t, int) and t == tiles - 1:
                    dve.wait_ge(s[("s4", "s6", "s8")[i]], tiles - R2)
                    nc.vector.memset(as_f32(zi[up, :, z_rows - 1, inner]), 0.0).then_inc(s[f"z{i}_edge"], 1)

            def step(g, j, k):
                t = k - 7
                if valid(t):
                    dve.wait_ge(s["f"], t + 1)
                    dve.wait_ge(s["x_scaled"], t + 1)
                    xt = sh.x[:, bass.ds(t * TILE, TILE)]
                    if out_dram is None:
                        nc.vector.tensor_tensor(xt, xt, ps_f[:, 0:TILE], ALU.add).then_inc(s["updated"], 1)
                        dve.wait_ge(s["updated"], t + 1)
                        nc.vector.bn_stats(sh.stats[:, bass.ds(t * 6, 6)], xt).then_inc(s["counted"], 1)
                    else:
                        dve.wait_ge(s["out_turned"], t + 1)
                        nc.vector.tensor_tensor(result, xt, ps_f[:, 0:TILE], ALU.add).then_inc(s["updated"], 1)
                t, jt = k - 6, j % BODY
                add_up(3, t, jt)
                if valid(t):
                    dve.wait_ge(s["r_hi"], t + 1)
                    nc.vector.scalar_tensor_tensor(r_lo[:, :], acc[:, jt, :], 0.0, as_f32(r_hi[:, :]),
                                                   ALU.max, ALU.subtract).then_inc(s["r_lo"], 1)
                add_up(2, k - 4, (j - 4) % BODY)
                low_z(2, g, j, 4)
                t = k - 7
                if out_dram is not None and valid(t):
                    dve.wait_ge(s["out_turned"], t + 2)
                    nc.vector.tensor_scalar(sh.x[:, bass.ds(t * TILE, TILE)], ps_out, 1.0, None, ALU.mult)\
                        .then_inc(s["out_kept"], 1)
                t, jt = k + 2, (j + 2) % BODY
                if valid(t):
                    dve.wait_ge(s["a_hi"], t + 1)
                    r0 = 1 + TR * (jt % R2)
                    nc.vector.tensor_tensor(a_lo[:, r0:r0 + TR, inner], grid(a_f[:, :]),
                                            as_f32(a_hi[:, r0:r0 + TR, inner]), ALU.subtract)\
                        .then_inc(s["a_lo"], 1)
                add_up(1, k - 2, (j - 2) % BODY)
                low_z(1, g, j, 2)
                low_z(0, g, j, 0)

            walk(dve, step)

        @block.tensor
        def _(pe):
            def dense(g, j, k, part):
                if not valid(k):
                    return
                if part == 0:
                    pe.wait_ge(s["a_hi"], k + 1)
                    pe.wait_ge(s["a_lo"], k + 1)
                    wait(pe, s["sum0"], k - 1)
                else:
                    pe.wait_ge(s["a_hi"], upto(k + 2))
                    pe.wait_ge(s["a_lo"], upto(k + 2))
                mirrored_for(g, j, part)
                out = grid(ps_d[j % 2][:, 0:TILE])
                r0 = 1 + TR * (j % R2)
                for n, (dy, dx) in list(enumerate(TAPS))[:5] if part == 0 else list(enumerate(TAPS))[5:]:
                    rows, cols = slice(r0 + dy, r0 + dy + TR), slice(1 + dx, 1 + dx + SIDE)
                    last = split_product(nc, out, u_hi[:, n, :], u_lo[:, n, :], a_hi[:, rows, cols],
                                         a_lo[:, rows, cols], start=n == 0, stop=n == 8)
                if part:
                    last.then_inc(s["s2"], 1)

            def mirrored_for(g, j, part):
                if j % R2 == 0 and part == 0:
                    pe.wait_ge(s["mirrored"], g * 4 + (j // R2) * 2 + 1)
                if j % R2 == R2 - 1 and part == 1:
                    pe.wait_ge(s["mirrored"], g * 4 + (j // R2) * 2 + 4)

            def add_block(i, g, j, lag, done):
                t, jt, gt = g * BODY + (j - lag), (j - lag) % BODY, group_of(g, j, lag)
                if not valid(t):
                    return
                pe.wait_ge(s[f"z{i}_lo"], upto(t + 2))
                if isinstance(t, int) and t == 0:
                    pe.wait_ge(z_copied[i][0], 32)
                if not isinstance(t, int) or t + 1 < tiles:
                    pe.wait_ge(z_copied[i][(jt + 1) % 2], gt * (16 * BODY) + 32 * ((jt + 1) // 2 + 1))
                if jt % R2 == 0:
                    wait(pe, s[f"z{i}_edge"], gt * 4 + jt // R2 * 2)
                if jt % R2 == R2 - 1:
                    pe.wait_ge(s[f"z{i}_edge"], gt * 4 + jt // R2 * 2 + 3)
                wait(pe, s[f"sum{i + 1}"], t)
                out = grid(ps_z[i][0:32 * (3 - i), 0:TILE])
                r0 = TR * (jt % R2)
                for dx in range(3):
                    zi = (z[i][:, half, r0:r0 + TR, dx:dx + SIDE] for half in range(2))
                    last = split_product(nc, out, v_hi[i][:, dx, :], v_lo[i][:, dx, :], *zi,
                                         start=dx == 0, stop=dx == 2)
                last.then_inc(s[done], 1)

            def step(g, j, k):
                dense(g, j, k, 0)
                add_block(2, g, j, 6, "s8")
                add_block(1, g, j, 4, "s6")
                t = k - 7
                if out_dram is not None and valid(t):
                    pe.wait_ge(s["updated"], t + 1)
                    pe.wait_ge(s["out_kept"], t + 1)
                    for q in range(TILE // P):
                        last = nc.tensor.transpose(ps_out[:, q * P:(q + 1) * P],
                                                   result[:, q * P:(q + 1) * P], sh.const[:, C_ID:C_ID + P])
                    last.then_inc(s["out_turned"], 1)
                t, i = k + 2, (j + 2) % 2
                if valid(t):
                    pe.wait_ge(s["xn_hi"], t + 1)
                    pe.wait_ge(s["xn_lo"], t + 1)
                    wait(pe, s["a_hi"], t)
                    split_product(nc, ps_a[:, 0:TILE], m1_hi[:, :], m1_lo[:, :], xn_hi[i][:, :],
                                  xn_lo[i][:, :]).then_inc(s["s1"], 1)
                add_block(0, g, j, 2, "s4")
                dense(g, j, k, 1)
                t = k - 6
                if valid(t):
                    pe.wait_ge(s["r_hi"], t + 1)
                    pe.wait_ge(s["r_lo"], t + 1)
                    wait(pe, s["updated"], t)
                    split_product(nc, ps_f[:, 0:TILE], m3_hi[:, :], m3_lo[:, :], r_hi[:, :],
                                  r_lo[:, :]).then_inc(s["f"], 1)

            walk(pe, step)


def program(nc, x, const, at_w, at_b, at_tables, c1_w, c1_b, bn, w2, w3, out):
    images = x.shape[0] // IMG
    with ExitStack() as ctx:
        sh = Shared(nc, ctx, images)
        y = nc.dram_tensor("y", [P, sh.tokens], F32, kind="Internal").ap()
        load_stage(sh, x, const)
        group_norm_stage(sh, "gn0", IMG // BANK)
        attention_stage(sh, at_w, at_b, at_tables)
        sh.recycle()
        group_norm_stage(sh, "gn1", TILES)
        conv1_stage(sh, c1_w, c1_b, y)
        batch_norm_stage(sh, bn, y)
        group_norm_stage(sh, "gn2", TILES)
        stack_stage(sh, "l2", w2)
        group_norm_stage(sh, "gn3", TILES)
        stack_stage(sh, "l3", w3, out)


def stacked_taps(w2):
    w2 = w2.reshape(3, 3, 4, 32, 32)
    out = np.zeros((3, 4, 32, 3, 32), np.float32)
    for i in range(3):
        for group, dy in enumerate(COPIES[i]):
            if dy is not None:
                out[i, group] = w2[1 + dy, :, i].transpose(1, 0, 2)
    return out.transpose(1, 2, 0, 3, 4).reshape(P, 288)


def pack_stack(w1, b1, w2, b2, w3, b3):
    out = np.zeros((P, W_END), np.float32)
    w1, w2, w3 = w1.reshape(P, 32), w2.reshape(3, 3, P, 32), w3.reshape(P)
    out[:, W_1:W_1B] = w1
    out[:32, W_1B:W_B1] = w1.reshape(4, 32, 32).transpose(1, 0, 2).reshape(32, P)
    out[:32, W_B1] = b1.reshape(32)
    out[:, W_2:W_2S] = w2.transpose(2, 0, 1, 3).reshape(P, 288)
    out[:, W_2S:W_B2] = stacked_taps(w2)
    out[:, W_B2] = np.tile(b2.reshape(32), 4)
    out[:, W_3R:W_3C] = w3[None]
    out[:, W_3C] = w3
    out[:, W_B3] = b3.reshape(1)
    return out


def kernel(**inputs):
    import concourse.bacc as bacc
    from concourse.bass_utils import run_bass_kernel_spmd

    x = np.asarray(inputs["x"])
    images = x.shape[0]
    wq, bq = np.asarray(inputs["L0_conv_W_qkv"]), np.asarray(inputs["L0_conv_b_qkv"])
    c = np.arange(P)
    partner = c + np.where(c % 8 < 4, 4, -4)
    even_odd = np.argsort(c // HD % 2, kind="stable")
    w = [wq[:, :P], wq[:, :P][:, partner], wq[:, P:2 * P], wq[:, P:2 * P][:, partner],
         wq[:, 2 * P:][:, even_odd], np.asarray(inputs["L0_conv_W_proj"])]
    b = [bq[:P], bq[:P][partner], bq[P:2 * P], bq[P:2 * P][partner], bq[2 * P:],
         np.asarray(inputs["L0_conv_b_proj"])]
    arrays = {
        "x": x.reshape(-1, P),
        "const": constants(images),
        "at_w": np.concatenate(w, 1),
        "at_b": np.stack(b, 1),
        "at_tables": attention_tables(),
        "c1_w": np.asarray(inputs["L1_conv_w"]).reshape(9, 4, P)[:, c % 4].transpose(1, 0, 2),
        "c1_b": np.asarray(inputs["L1_conv_b"])[:, None],
        "bn": np.stack([np.asarray(inputs[f"L1_conv_{n}"]) for n in ("gamma", "beta")], 1),
        "w2": pack_stack(*(np.asarray(inputs[f"L2_conv_{n}"]) for n in ("w1", "b1", "w2", "b2", "w3", "b3"))),
        "w3": pack_stack(*(np.asarray(inputs[f"L3_conv_{n}"]) for n in ("w1", "b1", "w2", "b2", "w3", "b3"))),
    }
    arrays = {f"in_{k}": np.ascontiguousarray(v) for k, v in arrays.items()}
    nc = bacc.Bacc("TRN2", target_bir_lowering=False, num_devices=1, dynamic_dma_scratch_size=1024)
    args = [nc.dram_tensor(k, v.shape, F32, kind="ExternalInput").ap() for k, v in arrays.items()]
    args.append(nc.dram_tensor("out", arrays["in_x"].shape, F32, kind="ExternalOutput").ap())
    program(nc, *args)
    r = run_bass_kernel_spmd(nc, [arrays], core_ids=[0])
    return r.results[0]["out"].reshape(x.shape)
```
